# Optimizing a Trainium2 kernel written in Bass

```python
import numpy as np
import jax
import jax.numpy as jnp

def _softmax(x, axis=-1):
    return jax.nn.softmax(x, axis=axis)

def _gelu(x):
    return jax.nn.gelu(x, approximate=True)

def _silu(x):
    return jax.nn.silu(x)

def _sigmoid(x):
    return jax.nn.sigmoid(x)

def _layernorm(x, axis=-1, eps=1e-05):
    m = jnp.mean(x, axis=axis, keepdims=True)
    v = jnp.var(x, axis=axis, keepdims=True)
    return (x - m) / jnp.sqrt(v + eps)

def _scatter_add(tgt, idx, src, axis=0):
    return tgt.at[idx].add(src)

def _segment_sum(src, seg, n):
    return jax.ops.segment_sum(src, seg, n)
kernel_name = 'mk_conv_preact_d2_conv_nchw256_r4_98800e'

def setup_inputs(seed: int=0):
    np.random.seed(seed)
    _w = jnp.asarray

    def _rec_inputs():
        import jax
        import jax.numpy as jnp
        _gk = jax.random.key(seed)
        x = -8.268e-05 + 0.9999 * jax.random.normal(jax.random.fold_in(_gk, 1), (16, 64, 56, 56), jnp.float32)
        return x
    x = _rec_inputs()

    def _L0_conv_setup():
        import jax, jax.numpy as jnp
        import numpy as np
        B, C, H, W = (16, 64, 56, 56)
        HEADS, DH, WS = (16, 16, 7)
        EPS = 1e-06
        key = jax.random.key(seed)
        k1, k2, k3 = jax.random.split(key, 3)
        return {'x': jax.random.normal(k1, (B, C, H, W), jnp.float32), 'bn_gamma': jnp.ones((C,), jnp.float32), 'bn_beta': jnp.zeros((C,), jnp.float32), 'bn_mean': jnp.zeros((C,), jnp.float32), 'bn_var': jnp.ones((C,), jnp.float32), 'qk_w': jax.random.normal(k2, (2 * C, C), jnp.float32) * 0.02, 'v_w': jax.random.normal(k3, (C, C), jnp.float32) * 0.02}
    _L0_conv_all = _L0_conv_setup()
    _L0_conv_in = {k: v for k, v in _L0_conv_all.items() if k in ('bn_gamma', 'bn_beta', 'bn_mean', 'bn_var', 'qk_w', 'v_w')}
    del _L0_conv_all

    def _L1_conv_setup():
        import jax, jax.numpy as jnp
        import numpy as np
        KSIZE = 5
        PAD = 2
        DILATE = 1
        STRIDE = 1
        NHEADS = 8

        def extract_patches(x, ksize=KSIZE, pad=PAD, dilate=DILATE, stride=STRIDE):
            N, D, H, W = x.shape
            xp = jnp.pad(x, ((0, 0), (0, 0), (pad, pad), (pad, pad)))
            Ho = (H + 2 * pad - dilate * (ksize - 1) - 1) // stride + 1
            Wo = (W + 2 * pad - dilate * (ksize - 1) - 1) // stride + 1
            slices = []
            for i in range(ksize):
                for j in range(ksize):
                    r0, c0 = (i * dilate, j * dilate)
                    slices.append(xp[:, :, r0:r0 + (Ho - 1) * stride + 1:stride, c0:c0 + (Wo - 1) * stride + 1:stride])
            return jnp.stack(slices, axis=2)
        key = jax.random.key(seed)
        k1, k2 = jax.random.split(key)
        N, D, H, W = (8, 64, 56, 56)
        outC = 64
        x = jax.random.normal(k1, (N, D, H, W), dtype=jnp.float32)
        w_out = jax.random.normal(k2, (outC, D), dtype=jnp.float32) * (1.0 / np.sqrt(D))
        b_out = jnp.zeros((outC,), dtype=jnp.float32)
        return {'x': x, 'w_out': w_out, 'b_out': b_out}
    _L1_conv_all = _L1_conv_setup()
    _L1_conv_in = {k: v for k, v in _L1_conv_all.items() if k in ('w_out', 'b_out')}
    del _L1_conv_all
    return {'x': x, 'L0_conv_bn_gamma': _L0_conv_in['bn_gamma'], 'L0_conv_bn_beta': _L0_conv_in['bn_beta'], 'L0_conv_bn_mean': _L0_conv_in['bn_mean'], 'L0_conv_bn_var': _L0_conv_in['bn_var'], 'L0_conv_qk_w': _L0_conv_in['qk_w'], 'L0_conv_v_w': _L0_conv_in['v_w'], 'L1_conv_w_out': _L1_conv_in['w_out'], 'L1_conv_b_out': _L1_conv_in['b_out']}

def reference(x, L0_conv_bn_gamma, L0_conv_bn_beta, L0_conv_bn_mean, L0_conv_bn_var, L0_conv_qk_w, L0_conv_v_w, L1_conv_w_out, L1_conv_b_out):
    import jax
    import jax.numpy as jnp

    def _L0_conv_ref(x, bn_gamma, bn_beta, bn_mean, bn_var, qk_w, v_w):
        import jax, jax.numpy as jnp
        import numpy as np
        B, C, H, W = (16, 64, 56, 56)
        HEADS, DH, WS = (16, 16, 7)
        EPS = 1e-06
        Bb, Cc, Hh, Ww = x.shape
        scale = DH ** (-0.5)
        inv = bn_gamma / jnp.sqrt(bn_var + EPS)
        xn = (x - bn_mean[:, None, None]) * inv[:, None, None] + bn_beta[:, None, None]
        n1, n2 = (Hh // WS, Ww // WS)
        t = xn.reshape(Bb, Cc, WS, n1, WS, n2).transpose(0, 3, 5, 2, 4, 1)
        tok = t.reshape(Bb * n1 * n2, WS * WS, Cc)
        qk = (tok @ qk_w.T).reshape(-1, WS * WS, 2, HEADS, DH)
        q = qk[:, :, 0].transpose(0, 2, 1, 3)
        k = qk[:, :, 1].transpose(0, 2, 1, 3)
        attn = jax.nn.softmax(jnp.einsum('bhqd,bhkd->bhqk', q, k) * scale, axis=-1)
        v = jax.nn.relu(tok @ v_w.T).reshape(-1, WS * WS, HEADS, DH).transpose(0, 2, 1, 3)
        o = jnp.einsum('bhqk,bhkd->bhqd', attn, v)
        o = o.transpose(0, 2, 1, 3).reshape(Bb, n1, n2, WS, WS, Cc)
        out = o.transpose(0, 5, 3, 1, 4, 2).reshape(Bb, Cc, Hh, Ww)
        return out

    def _L1_conv_ref(x, w_out, b_out):
        import jax, jax.numpy as jnp
        import numpy as np
        KSIZE = 5
        PAD = 2
        DILATE = 1
        STRIDE = 1
        NHEADS = 8

        def extract_patches(x, ksize=KSIZE, pad=PAD, dilate=DILATE, stride=STRIDE):
            N, D, H, W = x.shape
            xp = jnp.pad(x, ((0, 0), (0, 0), (pad, pad), (pad, pad)))
            Ho = (H + 2 * pad - dilate * (ksize - 1) - 1) // stride + 1
            Wo = (W + 2 * pad - dilate * (ksize - 1) - 1) // stride + 1
            slices = []
            for i in range(ksize):
                for j in range(ksize):
                    r0, c0 = (i * dilate, j * dilate)
                    slices.append(xp[:, :, r0:r0 + (Ho - 1) * stride + 1:stride, c0:c0 + (Wo - 1) * stride + 1:stride])
            return jnp.stack(slices, axis=2)
        N, D, H, W = x.shape
        K2 = KSIZE * KSIZE
        hdim = D // NHEADS
        patches = extract_patches(x)
        p = patches.reshape(N, NHEADS, hdim, K2, H, W)
        q = x.reshape(N, NHEADS, hdim, 1, H, W)
        scores = (p * q).sum(axis=2, keepdims=True)
        att = jax.nn.softmax(scores, axis=3)
        out = (p * att).sum(axis=3).reshape(N, D, H, W)
        out = jnp.einsum('ndhw,od->nohw', out, w_out) + b_out[None, :, None, None]
        return out

    def _gn(v, G=32, eps=1e-05):
        B_, C_, H_, W_ = v.shape
        g = v.reshape(B_, G, C_ // G, H_, W_)
        m = jnp.mean(g, axis=(2, 3, 4), keepdims=True)
        s = jnp.var(g, axis=(2, 3, 4), keepdims=True)
        return ((g - m) / jnp.sqrt(s + eps)).reshape(v.shape)

    def _ln_c(v, eps=1e-06):
        m = jnp.mean(v, axis=1, keepdims=True)
        s = jnp.var(v, axis=1, keepdims=True)
        return (v - m) / jnp.sqrt(s + eps)

    def _ln_t(v, eps=1e-05):
        m = jnp.mean(v, axis=-1, keepdims=True)
        s = jnp.var(v, axis=-1, keepdims=True)
        return (v - m) / jnp.sqrt(s + eps)

    def _to_tokens(v):
        B_, C_, H_, W_ = v.shape
        return v.reshape(B_, C_, H_ * W_).transpose(0, 2, 1)

    def _from_tokens(t, like):
        B_, C_, H_, W_ = like.shape
        return t.transpose(0, 2, 1).reshape(B_, C_, H_, W_)
    x = x + _L0_conv_ref(_gn(x), L0_conv_bn_gamma, L0_conv_bn_beta, L0_conv_bn_mean, L0_conv_bn_var, L0_conv_qk_w, L0_conv_v_w)
    x = x + _L1_conv_ref(_gn(x), L1_conv_w_out, L1_conv_b_out)
    return x

_drawn_inputs = setup_inputs


def setup_inputs(seed=0):
    import zlib

    import numpy as np

    out = dict(_drawn_inputs(seed))
    spreads = {'L0_conv_bn_gamma': (1.0, 0.6),
     'L0_conv_bn_beta': (0.0, 0.8),
     'L0_conv_bn_mean': (0.0, 0.8),
     'L0_conv_bn_var': (1.0, 0.6),
     'L1_conv_b_out': (0.0, 0.1)}
    factors = {'L0_conv_qk_w': 8.0, 'L0_conv_v_w': 3.025}
    for name, (base, spread) in spreads.items():
        noise = np.random.default_rng([zlib.crc32(name.encode()), seed]).standard_normal(out[name].shape)
        drawn = base * np.exp(spread * noise) if base else spread * noise
        out[name] = jnp.asarray(drawn.astype(out[name].dtype))
    for name, factor in factors.items():
        out[name] = (out[name] * factor).astype(out[name].dtype)
    return out
```

```python
from contextlib import ExitStack

import concourse.bass as bass
from concourse import mybir

F32 = mybir.dt.float32
ALU = mybir.AluOpType
ACT = mybir.ActivationFunctionType
AX_X = mybir.AxisListType.X

P = 128
B, C, H, W = 16, 64, 56, 56
HW = H * W
BP = B // 2
BANK = 512

WS = 7
NI = H // WS
S = WS * WS
SP = 64
ELT = 4 * S
UT = 2 * ELT
HEADS_R = 8
UNITS = BP * NI
VW = 48
ATT_SCALE = 16 ** -0.5
BN_EPS = 1e-6
GN_EPS = 1e-5

KS = 5
R = 2
RG = 8
GR = H // RG
HR = GR + 2 * R
WP = W + 2 * R
HALO = HR * WP
PIX = GR * W
LH = 8
HD = C // LH
NK = KS * KS
CH = HD // 2
TILE = CH * (GR + R) * (W + R)
HALF_PLANE = [(0, 0), (0, 1), (0, 2)] + [(dy, dx) for dy in (1, 2) for dx in range(-2, 3)]
ALL_SHIFTS = [(dy, dx) for dy in range(-2, 3) for dx in range(-2, 3)]


def slot_of(dy, dx):
    return (dy + R) * KS + dx + R


def region(dy, dx):
    rows = GR + dy
    c0 = min(R, R - dx)
    return R - dy, rows, c0, W + abs(dx)


def segments(rows, cols):
    if rows * cols <= BANK:
        return [(0, rows)]
    half = (rows + 1) // 2
    return [(0, half), (half, rows)]


DVE_SLOTS, POOL_SLOTS = 3, 2
PAIRED = 8
POOL_FULL, POOL_S, POOL_V = 18, 8, 12
EARLY_V = 5
LATE_S = 4
S_TILES = len(HALF_PLANE)
MAX_PARTS, SUB_PARTS = 4, KS


def spread(many, few):
    out, i, j = [], 0, 0
    while i < len(many) or j < len(few):
        if j >= len(few) or (i < len(many) and i * len(few) <= j * len(many)):
            out.append(many[i])
            i += 1
        else:
            out.append(few[j])
            j += 1
    return out


def value_tasks(half):
    ks, out = list(range(NK)), []
    while ks:
        n = 2 if len(out) % 2 == 0 and len(out) < 2 * PAIRED and len(ks) > 1 else 1
        out.append(("v", half, tuple(ks[:n])))
        ks = ks[n:]
    return out


def plan(scores, values, pool_tiles):
    s = [("s", t, a) for t in range(S_TILES) for a in range(2)] if scores else []
    v0, v1 = (value_tasks(0), value_tasks(1)) if values else ([], [])
    if scores and values:
        order = v0[:EARLY_V] + spread(s[:-LATE_S], v0[EARLY_V:]) + s[-LATE_S:] + v1
    else:
        order = s + v0 + v1
    free = [n for n, t in enumerate(order) if not (t[0] == "v" and len(t[2]) == 2)]
    pool = {free[(2 * k + 1) * len(free) // (2 * pool_tiles)] for k in range(pool_tiles)}
    assert len(pool) == pool_tiles
    return [("pool" if n in pool else "dve", t) for n, t in enumerate(order)]


FULL, ONLY_S, ONLY_V = plan(True, True, POOL_FULL), plan(True, False, POOL_S), plan(False, True, POOL_V)


def count(tiles, who):
    return sum(1 for w, _ in tiles if w == who)


for tiles in (FULL, ONLY_S):
    assert count(tiles, "dve") % DVE_SLOTS == 0 and count(tiles, "pool") % POOL_SLOTS == 0


def tiles_before(j, who):
    if isinstance(j, int) and j == 0:
        return 0
    return (j - 1) * count(FULL, who) + count(ONLY_S, who)


def build(nc, x, bn_gamma, bn_beta, bn_mean, bn_var, qk_w, v_w, w_out, b_out, out):
    halo_dram = nc.dram_tensor("halo_dram", (2, C, BP, RG, HALO), F32).ap()
    x1_dram = nc.dram_tensor("x1_dram", (2 * C, BP, HW), F32).ap()
    attn_dram = nc.dram_tensor("attn_dram", (2, C, BP, RG, PIX), F32).ap()
    x_rows = x.rearrange("(bp b2) c h w -> (b2 c) bp (h w)", b2=2)
    out_rows = out.rearrange("(bp b2) c h w -> (b2 c) bp (h w)", b2=2)
    attn_rows = attn_dram.rearrange("b2 c bp rg n -> (b2 c) bp (rg n)")

    with ExitStack() as ctx:
        def sem(name):
            return ctx.enter_context(nc.semaphore(name))

        consts = ctx.enter_context(nc.sbuf_tensor("consts", [P, 2600], F32))
        arena = ctx.enter_context(nc.sbuf_tensor("arena", [P, 50000], F32))
        PS = ctx.enter_context(nc.psum_tensor("PS", [P, 8, BANK], F32))

        used = [0, 0]

        def const(n):
            used[0] += n
            assert used[0] <= 2600
            return consts[:, used[0] - n:used[0]]

        def room(n):
            used[1] += n
            assert used[1] <= 50000, used[1]
            return arena[:, used[1] - n:used[1]]

        ident = const(P)
        pair_mean = const(P)
        head_mask = const(HEADS_R)
        w_nat = [const(P) for _ in range(4)]
        w_T_all = const(4 * P)
        w_T = [w_T_all[:, n * P:(n + 1) * P] for n in range(4)]
        wqk_T, wv_T, wout_T = w_T[0:2], w_T[2], w_T[3]
        par = const(5)
        bn_inv, bn_off = const(1), const(1)
        chunk_stats = const(BP * 7 * 6).rearrange("p (b k s) -> p b k s", b=BP, k=7)
        mean_var = const(BP * 2).rearrange("p (b s) -> p b s", s=2)
        g_mean, g_dev, g_std = const(BP), const(BP), const(BP)
        g_rstd, g_bias = const(BP), const(BP)
        t_scale, t_bias, t_tmp = const(BP), const(BP), const(BP)

        xs = room(BP * HW).rearrange("p (b n) -> p b n", b=BP)
        tok = [room(UT) for _ in range(2)]
        qk_sb = [[room(UT + SP) for _ in range(2)] for _ in range(2)]
        v_ch = [room(2 * 4 * SP).rearrange("p (e r s) -> p e r s", e=2, r=4) for _ in range(2)]
        k_bd = [room(2 * HEADS_R * S).rearrange("p (r h s) -> p r h s", r=2, h=HEADS_R) for _ in range(4)]
        v_bd = [[room(16 * VW).rearrange("p (g n) -> p g n", n=VW) for _ in range(2)] for _ in range(2)]
        probs = [room(HEADS_R * SP).rearrange("p (h s) -> p h s", s=SP) for _ in range(4)]
        row_max = [room(HEADS_R) for _ in range(2)]
        probs_T = [room(4 * P).rearrange("p (j n) -> p j n", j=4) for _ in range(2)]
        rden = [room(HEADS_R) for _ in range(2)]
        o_tok = [room(2 * 2 * 2 * C).rearrange("p (e u b c) -> p e u b c", b=2, e=2, u=2) for _ in range(2)]
        res = [room(UT) for _ in range(2)]
        window_end = used[1]
        padded = [room(WP * WP).rearrange("p (h w) -> p h w", w=WP) for _ in range(2)]
        assert window_end <= 50000

        used[1] = 0
        xh = [room(HD * HALO).rearrange("p (c h w) -> p c h w", c=HD, h=HR) for _ in range(2)]
        sc = [room(NK * PIX).rearrange("p (k n) -> p k n", k=NK) for _ in range(2)]
        dve_ring = [room(TILE) for _ in range(DVE_SLOTS)]
        dve_extra = room(CH * PIX)
        pool_ring = [room(TILE) for _ in range(POOL_SLOTS)]
        smax = room(PIX)
        lsum = room(PIX)
        lden = [room(PIX) for _ in range(2)]
        o_loc = [room(CH * PIX).rearrange("p (c n) -> p c n", c=CH) for _ in range(2)]
        used[1] = 0
        x1_in = [room(HW) for _ in range(3)]
        at_in = [room(HW) for _ in range(3)]
        fin = [room(HW) for _ in range(2)]

        x_loaded = [sem(f"x_loaded{i}") for i in range(BP)]
        par_loaded = sem("par_loaded")
        w_zeroed = sem("w_zeroed")
        masks_ready = sem("masks_ready")
        bufs_zeroed = sem("bufs_zeroed")
        w_transposed = sem("w_transposed")
        wT_ready = sem("wT_ready")
        st = sem("st")
        gn_in = sem("gn_in")
        gn_out = sem("gn_out")
        sq_in = sem("sq_in")
        sq_out = sem("sq_out")
        affine_ready = sem("affine_ready")
        tok_ready = sem("tok_ready")
        proj_done = sem("proj_done")
        proj_copied = sem("proj_copied")
        kbd_ready = sem("kbd_ready")
        vtr_done = sem("vtr_done")
        vbd_ready = sem("vbd_ready")
        s_done = sem("s_done")
        max_done = sem("max_done")
        sub_done = sem("sub_done")
        exp_done = sem("exp_done")
        pt_done = sem("pt_done")
        pt_copied = sem("pt_copied")
        pv_done = sem("pv_done")
        rden_done = sem("rden_done")
        norm_done = sem("norm_done")
        ot_done = sem("ot_done")
        res_ready = sem("res_ready")
        added = sem("added")
        pad_ready = sem("pad_ready")
        halo_stored = [sem("halo_stored0"), sem("halo_stored1")]
        x1_stored = sem("x1_stored")
        xh_loaded = [[sem(f"xh_loaded{s}{a}") for a in range(2)] for s in range(2)]
        dprod = sem("dprod")
        dprod_used = sem("dprod_used")
        pprod = sem("pprod")
        pprod_used = sem("pprod_used")
        dlink = sem("dlink")
        sc_copied = sem("sc_copied")
        lmax_done = sem("lmax_done")
        lsub_done = sem("lsub_done")
        lexp_done = sem("lexp_done")
        lden_done = sem("lden_done")
        lsum_done = sem("lsum_done")
        out_norm = sem("out_norm")
        o_stored = [sem("o_stored0"), sem("o_stored1")]
        fin_loaded = [sem(f"fin_loaded{i}") for i in range(3)]
        fproj = sem("fproj")
        fin_ready = sem("fin_ready")
        out_stored = [sem("out_stored0"), sem("out_stored1")]

        block = ctx.enter_context(nc.Block())

        def unit_pixels(u):
            off = (u // NI) * HW + (u % NI) * W
            first = arena[:, off:off + 1] if isinstance(u, int) else arena[:, bass.ds(off, 1)]
            return bass.AP(first.tensor, first.offset, [list(first.ap[0]), [1, NI], [NI * W, WS], [NI, WS]])

        def of_pair(t, u):
            return t[:, u // NI:u // NI + 1] if isinstance(u, int) else t[:, bass.ds(u // NI, 1)]

        def residue(buf, e, r):
            return buf[:, e * ELT + r:e * ELT + r + 4 * (SP - 1) + 1:4]

        def units(eng, unit, peel=1):
            for u in range(peel):
                unit(u, u % 2, u == 0, False)
            with eng.Fori(0, (UNITS - 1 - peel) // 2) as i:
                unit(peel + 2 * i, peel % 2, False, False)
                unit(peel + 1 + 2 * i, 1 - peel % 2, False, False)
            for u in range(peel + (UNITS - 1 - peel) // 2 * 2, UNITS):
                unit(u, u % 2, False, u == UNITS - 1)

        def heads(eng, iteration, looped=LH - 2):
            iteration(0, 0, True, False, ONLY_S)
            iteration(1, 1, True, True, FULL)
            with eng.Fori(0, looped // 2) as i:
                iteration(2 + 2 * i, 0, True, True, FULL)
                iteration(3 + 2 * i, 1, True, True, FULL)
            for j in range(2 + looped, LH):
                iteration(j, j % 2, True, True, FULL)
            iteration(LH, 0, False, True, ONLY_V)

        def multiply(eng, task, jp, buf):
            if task[0] == "s":
                _, t, a = task
                dy, dx = HALF_PLANE[t]
                r0, rows, c0, cols = region(dy, dx)
                X = xh[jp][:, a * CH:(a + 1) * CH]
                tile = buf[:, 0:CH * rows * cols].rearrange("p (c h w) -> p c h w", c=CH, h=rows)
                return [(tile, X[:, :, r0:r0 + rows, c0:c0 + cols],
                         X[:, :, r0 + dy:r0 + dy + rows, c0 + dx:c0 + dx + cols])]
            _, half, ks = task
            X = xh[1 - jp][:, half * CH:(half + 1) * CH]
            ops = []
            for dst, k in zip((buf[:, 0:CH * PIX], dve_extra), ks):
                dy, dx = ALL_SHIFTS[k]
                weight = sc[1 - jp][:, k, :].rearrange("p (h w) -> p h w", w=W)
                ops.append((dst.rearrange("p (c h w) -> p c h w", c=CH, h=GR),
                            X[:, :, R + dy:R + dy + GR, R + dx:R + dx + W],
                            weight.unsqueeze(1).to_broadcast([P, CH, GR, W])))
            return ops

        def await_sums(eng, j, tiles, match):
            last = max(n for n, (_, t) in enumerate(tiles) if match(t))
            who = tiles[last][0]
            eng.wait_ge(dprod_used if who == "dve" else pprod_used,
                        tiles_before(j, who) + count(tiles[:last + 1], who))

        def await_pixels(eng, jp, a, j):
            eng.wait_ge(xh_loaded[jp][a], 16 * (j - jp) + 32)

        @block.sync
        def _(sp):
            for bp in range(BP):
                sp.dma_start(xs[:, bp, :], x_rows[:, bp, :]).then_inc(x_loaded[bp], 16)
            sp.wait_ge(w_zeroed, 1)
            for b2 in range(2):
                rows = slice(b2 * C, (b2 + 1) * C)
                sp.dma_start(w_nat[b2][:, rows], qk_w).then_inc(par_loaded, 16)
                sp.dma_start(w_nat[2][rows, rows], v_w).then_inc(par_loaded, 16)
                sp.dma_start(w_nat[3][rows, rows], w_out).then_inc(par_loaded, 16)
                for n, v in enumerate((bn_gamma, bn_beta, bn_mean, bn_var, b_out)):
                    sp.dma_start(par[rows, n:n + 1], v.rearrange("(c o) -> c o", o=1)).then_inc(par_loaded, 16)

            sp.wait_ge(added, UNITS)
            for bp in range(BP):
                sp.dma_start(x1_dram[:, bp, :], xs[:, bp, :]).then_inc(x1_stored, 16)
            for bp in range(BP):
                sp.wait_ge(pad_ready, bp + 1)
                rows = padded[bp % 2].rearrange("p h w -> p (h w)")[:, 0:HALO]
                groups = bass.AP(rows.tensor, rows.offset, [list(rows.ap[0]), [GR * WP, RG], [1, HALO]])
                sp.dma_start(halo_dram.rearrange("b2 c bp rg n -> (b2 c) bp rg n")[:, bp],
                             groups).then_inc(halo_stored[bp % 2], 16)
            for q in halo_stored:
                sp.wait_ge(q, 16 * BP // 2)
            sp.wait_ge(x1_stored, 16 * BP)

            def load_half(j, jp, a):
                for b2 in range(2):
                    c0 = j * HD + a * CH
                    src = halo_dram[b2, c0:c0 + CH] if isinstance(j, int) else halo_dram[b2, bass.ds(c0, CH)]
                    sp.dma_start(xh[jp][b2 * C:(b2 + 1) * C, a * CH:(a + 1) * CH].rearrange("p c h w -> p c (h w)"),
                                 src.rearrange("c bp rg n -> (bp rg) c n")).then_inc(xh_loaded[jp][a], 16)

            def store_half(j, a):
                for b2 in range(2):
                    c0 = j * HD + a * CH
                    dst = attn_dram[b2, c0:c0 + CH] if isinstance(j, int) else attn_dram[b2, bass.ds(c0, CH)]
                    sp.dma_start(dst.rearrange("c bp rg n -> (bp rg) c n"),
                                 o_loc[a][b2 * C:(b2 + 1) * C]).then_inc(o_stored[a], 16)

            for j in range(2):
                for a in range(2):
                    load_half(j, j, a)

            def iteration(j, jp, do_s, do_v, tiles):
                if do_v:
                    for a in range(2):
                        sp.wait_ge(out_norm, 2 * (j - 1) + a + 1)
                        store_half(j - 1, a)
                        if not isinstance(j, int) or j + 1 < LH:
                            load_half(j + 1, 1 - jp, a)
            heads(sp, iteration, LH - 4)
            for q in o_stored:
                sp.wait_ge(q, 32 * LH)

            def load_pair(bp):
                sp.dma_start(at_in[bp % 3], attn_rows[:, bp, :]).then_inc(fin_loaded[bp % 3], 16)
                sp.dma_start(x1_in[bp % 3], x1_dram[:, bp, :]).then_inc(fin_loaded[bp % 3], 16)
            for bp in range(3):
                load_pair(bp)
            for bp in range(BP):
                sp.wait_ge(fin_ready, 2 * bp + 2)
                sp.dma_start(out_rows[:, bp, :], fin[bp % 2]).then_inc(out_stored[bp % 2], 16)
                if bp + 3 < BP:
                    load_pair(bp + 3)
            for q in out_stored:
                sp.wait_ge(q, 16 * BP // 2)

        @block.gpsimd
        def _(pool):
            for w in w_nat:
                i = nc.gpsimd.memset(w, 0.0)
            i.then_inc(w_zeroed, 1)
            nc.gpsimd.memset(ident, 0.0)
            nc.gpsimd.memset(pair_mean, 0.5)
            nc.gpsimd.memset(head_mask, 1.0).then_inc(masks_ready, 1)
            pool.wait_ge(masks_ready, 1)
            nc.gpsimd.affine_select(out=ident, in_=ident, compare_op=ALU.not_equal, fill=1.0, base=0,
                                    pattern=[[-1, P]], channel_multiplier=1)
            groups = pair_mean.rearrange("p (j k) -> p j k", k=2)
            nc.gpsimd.affine_select(out=groups, in_=groups, compare_op=ALU.is_ge, fill=0.0, base=0,
                                    pattern=[[-2, C], [0, 2]], channel_multiplier=1)
            slots = head_mask.rearrange("p (j h) -> p j h", h=2)
            nc.gpsimd.affine_select(out=slots, in_=slots, compare_op=ALU.is_ge, fill=0.0, base=0,
                                    pattern=[[-16, 4], [-64, 2]], channel_multiplier=1).then_inc(masks_ready, 1)
            pool.wait_ge(masks_ready, 2)
            nc.gpsimd.affine_select(out=groups, in_=groups, compare_op=ALU.is_ge, fill=0.0, base=1,
                                    pattern=[[2, C], [0, 2]], channel_multiplier=-1)
            nc.gpsimd.affine_select(out=slots, in_=slots, compare_op=ALU.is_ge, fill=0.0, base=15,
                                    pattern=[[16, 4], [64, 2]], channel_multiplier=-1).then_inc(masks_ready, 1)
            pool.wait_ge(masks_ready, 3)
            for u in range(2):
                for b2 in range(2):
                    nc.gpsimd.memset(qk_sb[u][b2][:, UT:UT + SP], 0.0)
                    nc.gpsimd.memset(v_bd[u][b2], 0.0)
                nc.gpsimd.memset(v_ch[u], 0.0)
            for q in probs + padded:
                i = nc.gpsimd.memset(q, 0.0)
            i.then_inc(bufs_zeroed, 1)
            pool.wait_ge(bufs_zeroed, 1)
            for u in range(2):
                for e in range(2):
                    nc.gpsimd.memset(v_bd[u][e][0:SP, :, 32:33], 1.0)
                    i = nc.gpsimd.memset(v_bd[u][e][SP:P, :, 33:34], 1.0)
            i.then_inc(bufs_zeroed, 1)

            def expand_keys(k, up):
                b2, e = k // 2, k % 2
                for r in range(2):
                    keys = residue(qk_sb[up][b2], e, 2 + r)[:, 0:S]
                    i = nc.gpsimd.tensor_tensor(k_bd[k][:, r], keys.unsqueeze(1).to_broadcast([P, HEADS_R, S]),
                                                head_mask.unsqueeze(2).to_broadcast([P, HEADS_R, S]), ALU.mult)
                i.then_inc(kbd_ready, 1)

            def add_residual(u, up):
                pool.wait_ge(res_ready, 2 * u + 2)
                v = unit_pixels(u)
                nc.gpsimd.tensor_tensor(v, v, res[up].rearrange("p (i a c) -> p i a c", i=NI, a=WS),
                                        ALU.add).then_inc(added, 1)

            def unit(u, up, first, last):
                for k in range(4):
                    if k % 2 == 0:
                        pool.wait_ge(proj_copied, 3 * u + k // 2 + 1)
                    if not first:
                        pool.wait_ge(s_done, 4 * u + k - 3)
                    expand_keys(k, up)
                    if k == 1 and not (isinstance(u, int) and u < 2):
                        add_residual(u - 2, up)
            units(pool, unit, peel=2)
            add_residual(UNITS - 2, 0)
            add_residual(UNITS - 1, 1)

            pool.wait_ge(x1_stored, 16 * BP)

            def iteration(j, jp, do_s, do_v, tiles):
                n, before = 0, tiles_before(j, "pool")
                seen = set()
                if do_v:
                    pool.wait_ge(lexp_done, SUB_PARTS * j)
                for who, task in tiles:
                    if who != "pool":
                        continue
                    if task[0] == "s" and task[2] not in seen:
                        seen.add(task[2])
                        await_pixels(pool, jp, task[2], j)
                    if not (isinstance(j, int) and j == 0 and n < POOL_SLOTS):
                        pool.wait_ge(pprod_used, before + n + 1 - POOL_SLOTS)
                    (o, a, b), = multiply(pool, task, jp, pool_ring[n % POOL_SLOTS])
                    nc.gpsimd.tensor_tensor(o, a, b, ALU.mult).then_inc(pprod, 1)
                    n += 1
            heads(pool, iteration)

        @block.scalar
        def _(act):
            act.wait_ge(wT_ready, 1)
            nc.scalar.activation(bn_inv, bn_off, ACT.Sqrt).then_inc(sq_out, 1)
            act.wait_ge(sq_in, 1)
            nc.scalar.activation(g_dev, g_std, ACT.Sqrt).then_inc(sq_out, 1)
            act.wait_ge(affine_ready, 1)
            act.wait_ge(bufs_zeroed, 2)

            def gather(u, up):
                nc.scalar.activation(tok[up].rearrange("p (i a c) -> p i a c", i=NI, a=WS), unit_pixels(u),
                                     ACT.Identity, bias=of_pair(t_bias, u), scale=of_pair(t_scale, u)
                                     ).then_inc(tok_ready, 1)

            def copy_qk(u, up, b2):
                act.wait_ge(proj_done, 3 * u + b2 + 1)
                nc.scalar.activation(qk_sb[up][b2][:, 0:UT], PS[:, 0, 0:UT], ACT.Copy).then_inc(proj_copied, 1)

            def copy_v(u, up):
                act.wait_ge(proj_done, 3 * u + 3)
                nc.scalar.activation(v_ch[up][:, :, :, 0:S], PS[:, 0, 0:UT].rearrange("p (e s r) -> p e r s", e=2, r=4),
                                     ACT.Relu).then_inc(proj_copied, 1)

            def place_values(u, up, e):
                act.wait_ge(vtr_done, 2 * u + e + 1)
                groups = PS[:, 1, 0:2 * P].rearrange("p (g n) -> p g n", n=16)
                for h in range(2):
                    rows = slice(h * SP, h * SP + S)
                    i = nc.scalar.activation(v_bd[up][e][rows, :, h * 16:h * 16 + 16], groups[rows], ACT.Copy)
                i.then_inc(vbd_ready, 1)

            def exponentials(n, k):
                act.wait_ge(sub_done, n + 1)
                nc.scalar.activation(probs[k][:, :, 0:S], probs[k][:, :, 0:S], ACT.Exp,
                                     scale=ATT_SCALE).then_inc(exp_done, 1)

            def copy_transposed(n, k, ready=True):
                act.wait_ge(pt_done, n + 1)
                if not (isinstance(n, int) and n < 2):
                    act.wait_ge(pv_done, n - 1)
                nc.scalar.activation(probs_T[k % 2].rearrange("p j n -> p (j n)"), PS[:, 4 + k % 2, :],
                                     ACT.Copy).then_inc(pt_copied, 1)

            gather(0, 0)
            for b2 in range(2):
                copy_qk(0, 0, b2)
            copy_v(0, 0)

            def unit(u, up, first, last):
                for k in range(4):
                    n = 4 * u + k
                    if not (first and k == 0):
                        copy_transposed(n - 1, (k - 1) % 4)
                    exponentials(n, k)
                    if k < 2:
                        place_values(u, up, k)
                    if not last:
                        if k == 0:
                            gather(u + 1, 1 - up)
                        elif k < 3:
                            copy_qk(u + 1, 1 - up, k - 1)
                        else:
                            copy_v(u + 1, 1 - up)
            units(act, unit)
            copy_transposed(4 * UNITS - 1, 3)

            act.wait_ge(sq_in, 2)
            nc.scalar.activation(g_dev, g_std, ACT.Sqrt).then_inc(sq_out, 1)
            act.wait_ge(affine_ready, 2)
            for bp in range(BP):
                if bp >= 2:
                    act.wait_ge(halo_stored[bp % 2], 16 * (bp // 2))
                nc.scalar.activation(padded[bp % 2][:, R:R + H, R:R + W], xs[:, bp, :].rearrange("p (h w) -> p h w", w=W),
                                     ACT.Identity, bias=g_bias[:, bp:bp + 1], scale=g_rstd[:, bp:bp + 1]
                                     ).then_inc(pad_ready, 1)

            def copy_scores(j, jp, t, tiles):
                await_sums(act, j, tiles, lambda task: task[:2] == ("s", t))
                dy, dx = HALF_PLANE[t]
                r0, rows, c0, cols = region(dy, dx)
                segs = segments(rows, cols)
                for sy, sx, py, px in {(dy, dx, 0, 0), (-dy, -dx, -dy, -dx)}:
                    top, left = R + py - r0, R + px - c0
                    dst = sc[jp][:, slot_of(sy, sx), :].rearrange("p (h w) -> p h w", w=W)
                    for s, (a, b) in enumerate(segs):
                        lo, hi = max(a, top), min(b, top + GR)
                        if lo >= hi:
                            continue
                        src = PS[:, 2 * (t % 2) + s, 0:(b - a) * cols].rearrange("p (h w) -> p h w", w=cols)
                        i = nc.scalar.activation(dst[:, lo - top:hi - top], src[:, lo - a:hi - a, left:left + W],
                                                 ACT.Copy)
                i.then_inc(sc_copied, 1)

            def iteration(j, jp, do_s, do_v, tiles):
                if not do_s:
                    return
                if isinstance(j, int) and j == 0:
                    act.wait_ge(x1_stored, 16 * BP)
                else:
                    act.wait_ge(dprod, tiles_before(j, "dve"))
                    act.wait_ge(pprod, tiles_before(j, "pool"))
                for t in range(S_TILES):
                    copy_scores(j, jp, t, tiles)
                for m in range(SUB_PARTS):
                    act.wait_ge(lsub_done, SUB_PARTS * j + m + 1)
                    v = sc[jp][:, m * KS:(m + 1) * KS, :].rearrange("p k n -> p (k n)")
                    nc.scalar.activation(v, v, ACT.Exp).then_inc(lexp_done, 1)
            heads(act, iteration)

        @block.vector
        def _(dve):
            steps = [0]

            def step(i):
                steps[0] += 1
                i.then_inc(st, 1)
                dve.wait_ge(st, steps[0])

            def group_stats(turn, ready):
                for bp in range(BP):
                    ready(bp)
                    for k in range(7):
                        i = nc.vector.bn_stats(chunk_stats[:, bp, k, :], xs[:, bp, k * 448:(k + 1) * 448])
                step(i)
                for bp in range(BP):
                    i = nc.vector.bn_aggr(mean_var[:, bp, :], chunk_stats[:, bp].rearrange("p k s -> p (k s)"))
                step(i)
                nc.vector.tensor_copy(t_tmp, mean_var[:, :, 0]).then_inc(gn_in, 1)
                dve.wait_ge(gn_out, 2 * turn + 1)
                step(nc.vector.tensor_copy(g_mean, PS[:, 0, 0:BP]))
                step(nc.vector.tensor_tensor(g_dev, mean_var[:, :, 0], g_mean, ALU.subtract))
                step(nc.vector.tensor_tensor(g_std, g_dev, g_dev, ALU.mult))
                nc.vector.tensor_tensor(t_tmp, g_std, mean_var[:, :, 1], ALU.add).then_inc(gn_in, 1)
                dve.wait_ge(gn_out, 2 * turn + 2)
                nc.vector.tensor_scalar(g_std, PS[:, 0, 0:BP], GN_EPS, None, ALU.add).then_inc(sq_in, 1)
                dve.wait_ge(sq_out, turn + 2)
                step(nc.vector.reciprocal(g_rstd, g_dev))
                step(nc.vector.scalar_tensor_tensor(out=g_bias, in0=g_mean, scalar=-1.0, in1=g_rstd,
                                                    op0=ALU.mult, op1=ALU.mult))

            dve.wait_ge(par_loaded, 16 * 16)
            nc.vector.tensor_scalar(bn_off, par[:, 3:4], BN_EPS, None, ALU.add).then_inc(wT_ready, 1)
            dve.wait_ge(w_transposed, 1)
            nc.vector.tensor_copy(w_T_all, PS[:, 1, :]).then_inc(wT_ready, 1)
            dve.wait_ge(sq_out, 1)
            step(nc.vector.reciprocal(bn_off, bn_inv))
            step(nc.vector.tensor_tensor(bn_inv, bn_off, par[:, 0:1], ALU.mult))
            step(nc.vector.tensor_tensor(t_tmp[:, 0:1], par[:, 2:3], bn_inv, ALU.mult))
            step(nc.vector.tensor_tensor(bn_off, par[:, 1:2], t_tmp[:, 0:1], ALU.subtract))
            group_stats(0, lambda bp: dve.wait_ge(x_loaded[bp], 16))
            nc.vector.tensor_scalar(t_scale, g_rstd, bn_inv, None, ALU.mult)
            nc.vector.tensor_scalar(t_bias, g_bias, bn_inv, bn_off, ALU.mult, ALU.add).then_inc(affine_ready, 1)
            dve.wait_ge(bufs_zeroed, 2)

            def subtract_max(n, k):
                bank = PS[:, 2 + k % 2, :].rearrange("p (h s) -> p h s", s=SP)[:, :, 0:S]
                dve.wait_ge(s_done, n + 1)
                nc.vector.tensor_reduce(row_max[k % 2], bank, AX_X, ALU.max).then_inc(max_done, 1)
                dve.wait_ge(max_done, n + 1)
                if not (isinstance(n, int) and n < 4):
                    dve.wait_ge(pt_done, n - 3)
                nc.vector.tensor_tensor(probs[k][:, :, 0:S], bank,
                                        row_max[k % 2].unsqueeze(2).to_broadcast([P, HEADS_R, S]),
                                        ALU.subtract).then_inc(sub_done, 1)

            def normalise(n, k, up):
                b2, e = k // 2, k % 2
                rd = rden[k % 2].rearrange("p (j q) -> p j q", q=2)
                o = PS[:, 6, 0:8 * VW].rearrange("p (j r n) -> p j r n", j=4, r=2)
                dve.wait_ge(pv_done, n + 1)
                nc.vector.reciprocal(rd, o[:, :, 0, 32:34]).then_inc(rden_done, 1)
                dve.wait_ge(rden_done, n + 1)
                for r in range(2):
                    rows = slice(r * SP, (r + 1) * SP)
                    dst = o_tok[up][rows, e, :, b2, :].rearrange("p q (j d) -> p j q d", j=4)
                    i = nc.vector.tensor_tensor(dst, o[rows, :, r, 0:32].rearrange("p j (q d) -> p j q d", q=2),
                                                rd[rows].unsqueeze(3).to_broadcast([SP, 4, 2, 16]), ALU.mult)
                i.then_inc(norm_done, 1)

            def order_tokens(u, up):
                dve.wait_ge(ot_done, u + 1)
                if not (isinstance(u, int) and u < 2):
                    dve.wait_ge(added, u - 1)
                for e in range(2):
                    src = PS[:, 7, e * 2 * P:(e + 1) * 2 * P].rearrange("p (h r s) -> p h r s", h=2, r=2)[:, :, :, 0:S]
                    dst = res[up][:, e * ELT:(e + 1) * ELT].rearrange("p (s r h) -> p h r s", r=2, h=2)
                    nc.vector.tensor_copy(dst, src).then_inc(res_ready, 1)

            def unit(u, up, first, last):
                for k in range(4):
                    n = 4 * u + k
                    subtract_max(n, k)
                    if not (first and k < 2):
                        normalise(n - 2, (k - 2) % 4, up if k >= 2 else 1 - up)
                    if k == 3 and not first:
                        order_tokens(u - 1, 1 - up)
            units(dve, unit, peel=3)
            normalise(4 * UNITS - 2, 2, 1)
            normalise(4 * UNITS - 1, 3, 1)
            order_tokens(UNITS - 1, 1)

            dve.wait_ge(added, UNITS)
            group_stats(1, lambda bp: None)
            nc.vector.tensor_copy(t_tmp, g_bias).then_inc(affine_ready, 1)

            pairs_full = sum(1 for _, t in FULL if t[0] == "v" and len(t[2]) == 2)

            def norm_half(j, jp, a, tiles):
                await_sums(dve, j, tiles, lambda task: task[:2] == ("v", a))
                if not (isinstance(j, int) and j == 1):
                    dve.wait_ge(o_stored[a], 32 * (j - 1))
                nc.vector.tensor_tensor(o_loc[a], PS[:, 4:8, 0:PIX],
                                        lden[1 - jp].unsqueeze(1).to_broadcast([P, CH, PIX]),
                                        ALU.mult).then_inc(out_norm, 1)

            def softmax_steps(j, jp):
                w = PIX // MAX_PARTS
                for m in range(MAX_PARTS):
                    def step_max(m=m):
                        if m == 0:
                            dve.wait_ge(sc_copied, S_TILES * (j + 1))
                        nc.vector.tensor_reduce(smax[:, m * w:(m + 1) * w],
                                                sc[jp][:, :, m * w:(m + 1) * w].rearrange("p k n -> p n k"),
                                                AX_X, ALU.max).then_inc(lmax_done, 1)
                    yield step_max
                for m in range(SUB_PARTS):
                    def step_sub(m=m):
                        if m == 0:
                            dve.wait_ge(lmax_done, MAX_PARTS * (j + 1))
                        v = sc[jp][:, m * KS:(m + 1) * KS, :]
                        nc.vector.tensor_tensor(v, v, smax.unsqueeze(1).to_broadcast([P, KS, PIX]),
                                                ALU.subtract).then_inc(lsub_done, 1)
                    yield step_sub
                for m in range(MAX_PARTS):
                    def step_sum(m=m):
                        if m == 0:
                            dve.wait_ge(lexp_done, SUB_PARTS * (j + 1))
                        nc.vector.tensor_reduce(lsum[:, m * w:(m + 1) * w],
                                                sc[jp][:, :, m * w:(m + 1) * w].rearrange("p k n -> p n k"),
                                                AX_X, ALU.add).then_inc(lsum_done, 1)
                    yield step_sum

                def step_inverse():
                    dve.wait_ge(lsum_done, MAX_PARTS * (j + 1))
                    nc.vector.reciprocal(lden[jp], lsum).then_inc(lden_done, 1)
                yield step_inverse

            def iteration(j, jp, do_s, do_v, tiles):
                n, before = 0, tiles_before(j, "dve")
                seen = set()
                pairs = 0
                pairs_before = 0 if isinstance(j, int) and j < 2 else (j - 1) * pairs_full
                soft = list(softmax_steps(j, jp)) if do_s else []
                last_s = max([i for i, (_, t) in enumerate(tiles) if t[0] == "s"], default=0)
                last_v0 = max([i for i, (_, t) in enumerate(tiles) if t[0] == "v" and t[1] == 0], default=0)
                if do_v:
                    dve.wait_ge(lden_done, j)
                for i, (who, task) in enumerate(tiles):
                    if do_v and i == last_v0 + 3:
                        norm_half(j, jp, 0, tiles)
                    if do_s and i > last_s + 1 and soft:
                        soft.pop(0)()
                    if who != "dve":
                        continue
                    if task[0] == "s" and task[2] not in seen:
                        seen.add(task[2])
                        await_pixels(dve, jp, task[2], j)
                    if not (isinstance(j, int) and j == 0 and n < DVE_SLOTS):
                        dve.wait_ge(dprod_used, before + n + 1 - DVE_SLOTS)
                    buf = dve_ring[n % DVE_SLOTS]
                    ops = multiply(dve, task, jp, buf)
                    if len(ops) == 1:
                        nc.vector.tensor_tensor(*ops[0], ALU.mult).then_inc(dprod, 1)
                    else:
                        nc.vector.tensor_tensor(*ops[0], ALU.mult).then_inc(dlink, 1)
                        dve.wait_ge(dprod, before + n)
                        nc.vector.tensor_tensor(*ops[1], ALU.mult).then_inc(dlink, 1)
                        pairs += 1
                        dve.wait_ge(dlink, 2 * (pairs_before + pairs))
                        nc.vector.tensor_tensor(buf[:, 0:CH * PIX], buf[:, 0:CH * PIX], dve_extra,
                                                ALU.add).then_inc(dprod, 1)
                    n += 1
                for s in soft:
                    s()
                if do_v:
                    norm_half(j, jp, 1, tiles)
            heads(dve, iteration)

            for bp in range(BP):
                dve.wait_ge(fin_loaded[bp % 3], 32 * (bp // 3 + 1))
                if bp >= 2:
                    dve.wait_ge(out_stored[bp % 2], 16 * (bp // 2))
                for g in range(2):
                    dve.wait_ge(fproj, 2 * bp + g + 1)
                    cols = slice(g * 4 * PIX, (g + 1) * 4 * PIX)
                    nc.vector.scalar_tensor_tensor(
                        out=fin[bp % 2][:, cols].rearrange("p (k n) -> p k n", k=4), in0=PS[:, 4 * g:4 * g + 4, 0:PIX],
                        scalar=par[:, 4:5], in1=x1_in[bp % 3][:, cols].rearrange("p (k n) -> p k n", k=4),
                        op0=ALU.add, op1=ALU.add).then_inc(fin_ready, 1)

        @block.tensor
        def _(pe):
            pe.wait_ge(masks_ready, 3)
            pe.wait_ge(par_loaded, 16 * 16)
            for n, w in enumerate(w_nat):
                i = nc.tensor.transpose(PS[:, 1, n * P:(n + 1) * P], w, ident)
            i.then_inc(w_transposed, 1)

            def pair_means(turn):
                for k in range(2):
                    pe.wait_ge(gn_in, 2 * turn + k + 1)
                    nc.tensor.matmul(PS[:, 0, 0:BP], pair_mean, t_tmp, start=True, stop=True).then_inc(gn_out, 1)

            pair_means(0)
            pe.wait_ge(wT_ready, 2)

            def project_qk(u, up, b2):
                if b2 == 0:
                    pe.wait_ge(tok_ready, u + 1)
                if not (isinstance(u, int) and u == 0 and b2 == 0):
                    pe.wait_ge(proj_copied, 3 * u + b2)
                nc.tensor.matmul(PS[:, 0, 0:UT], wqk_T[b2], tok[up], start=True, stop=True).then_inc(proj_done, 1)

            def project_v(u, up):
                pe.wait_ge(proj_copied, 3 * u + 2)
                nc.tensor.matmul(PS[:, 0, 0:UT], wv_T, tok[up], start=True, stop=True).then_inc(proj_done, 1)

            def transpose_v(u, up, e):
                pe.wait_ge(proj_copied, 3 * u + 3)
                if not (isinstance(u, int) and u == 0 and e == 0):
                    pe.wait_ge(vbd_ready, 2 * u + e)
                for r in range(2):
                    i = nc.tensor.transpose(PS[:, 1, r * P:(r + 1) * P],
                                            v_ch[up][:, e, 2 * r:2 * r + 2, :].rearrange("p r s -> p (r s)"), ident)
                i.then_inc(vtr_done, 1)

            def scores(n, k, up):
                b2, e = k // 2, k % 2
                pe.wait_ge(kbd_ready, n + 1)
                if not (isinstance(n, int) and n < 2):
                    pe.wait_ge(sub_done, n - 1)
                for r in range(2):
                    dst = PS[r * SP:(r + 1) * SP, 2 + k % 2, :].rearrange("p (h s) -> p h s", s=SP)[:, :, 0:S]
                    i = nc.tensor.matmul(dst, residue(qk_sb[up][b2], e, r), k_bd[k][:, r], start=True, stop=True)
                i.then_inc(s_done, 1)

            def transpose_probs(n, k):
                pe.wait_ge(exp_done, n + 1)
                if not (isinstance(n, int) and n < 2):
                    pe.wait_ge(pt_copied, n - 1)
                for j in range(4):
                    i = nc.tensor.transpose(PS[:, 4 + k % 2, j * P:(j + 1) * P],
                                            probs[k][:, 2 * j:2 * j + 2, :].rearrange("p h s -> p (h s)"), ident)
                i.then_inc(pt_done, 1)

            def weigh_values(n, k, up, vbd):
                b2, e = k // 2, k % 2
                pe.wait_ge(pt_copied, n + 1)
                pe.wait_ge(vbd_ready, vbd)
                if not (isinstance(n, int) and n == 0):
                    pe.wait_ge(norm_done, n)
                for j in range(4):
                    g = b2 * 4 + j
                    i = nc.tensor.matmul(PS[:, 6, 2 * VW * j:2 * VW * (j + 1)], probs_T[k % 2][:, j, :],
                                         v_bd[up][e][:, g:g + 9:8, :], start=True, stop=True)
                i.then_inc(pv_done, 1)

            def transpose_output(u, up):
                pe.wait_ge(norm_done, 4 * u + 4)
                if not (isinstance(u, int) and u == 0):
                    pe.wait_ge(res_ready, 2 * u)
                for e in range(2):
                    for h in range(2):
                        q = 2 * e + h
                        i = nc.tensor.transpose(PS[:, 7, q * P:(q + 1) * P], o_tok[up][:, e, h].rearrange("p b c -> p (b c)"), ident)
                i.then_inc(ot_done, 1)

            for b2 in range(2):
                project_qk(0, 0, b2)
            project_v(0, 0)

            def unit(u, up, first, last):
                for k in range(4):
                    n = 4 * u + k
                    scores(n, k, up)
                    if k < 2:
                        transpose_v(u, up, k)
                    if not (first and k == 0):
                        transpose_probs(n - 1, (k - 1) % 4)
                    if not (first and k < 2):
                        m = (k - 2) % 4
                        weigh_values(n - 2, m, up if k >= 2 else 1 - up,
                                     2 * u + m % 2 + 1 - (0 if k >= 2 else 2))
                    if not last:
                        if k in (1, 2):
                            project_qk(u + 1, 1 - up, k - 1)
                        elif k == 3:
                            project_v(u + 1, 1 - up)
                    if k == 3 and not first:
                        transpose_output(u - 1, 1 - up)
            units(pe, unit)
            transpose_probs(4 * UNITS - 1, 3)
            for k in (2, 3):
                weigh_values(4 * UNITS - 4 + k, k, 1, 2 * UNITS)
            transpose_output(UNITS - 1, 1)
            pair_means(1)

            def iteration(j, jp, do_s, do_v, tiles):
                made = {"dve": tiles_before(j, "dve"), "pool": tiles_before(j, "pool")}
                n = {"dve": 0, "pool": 0}
                vs = [[t for _, t in tiles if t[0] == "v" and t[1] == a] for a in range(2)]
                for who, task in tiles:
                    ring, slots, ready, used_up = (dve_ring, DVE_SLOTS, dprod, dprod_used) if who == "dve" else \
                        (pool_ring, POOL_SLOTS, pprod, pprod_used)
                    buf = ring[n[who] % slots]
                    n[who] += 1
                    pe.wait_ge(ready, made[who] + n[who])
                    if task[0] == "s":
                        _, t, a = task
                        _, rows, _, cols = region(*HALF_PLANE[t])
                        if a == 0 and not (isinstance(j, int) and j == 0 and t < 2):
                            pe.wait_ge(sc_copied, S_TILES * j + t - 1)
                        for c in range(CH):
                            for s, (lo, hi) in enumerate(segments(rows, cols)):
                                i = nc.tensor.matmul(
                                    PS[:, 2 * (t % 2) + s, 0:(hi - lo) * cols], ident,
                                    buf[:, (c * rows + lo) * cols:(c * rows + hi) * cols],
                                    start=(a == 0 and c == 0), stop=(a == 1 and c == CH - 1))
                        i.then_inc(used_up, 1)
                    else:
                        _, half, ks = task
                        first, last = task == vs[half][0], task == vs[half][-1]
                        if first and not (isinstance(j, int) and j == 1 and half == 0):
                            pe.wait_ge(out_norm, 2 * (j - 1) + half)
                        for c in range(CH):
                            i = nc.tensor.matmul(PS[:, 4 + c, 0:PIX], ident, buf[:, c * PIX:(c + 1) * PIX],
                                                 start=first, stop=last)
                        i.then_inc(used_up, 1)
            heads(pe, iteration)

            for bp in range(BP):
                pe.wait_ge(fin_loaded[bp % 3], 32 * (bp // 3 + 1))
                for g in range(2):
                    if bp:
                        pe.wait_ge(fin_ready, 2 * bp + g - 1)
                    for k in range(4 * g, 4 * g + 4):
                        i = nc.tensor.matmul(PS[:, k, 0:PIX], wout_T, at_in[bp % 3][:, k * PIX:(k + 1) * PIX],
                                             start=True, stop=True)
                    i.then_inc(fproj, 1)


_INS = ["x", "L0_conv_bn_gamma", "L0_conv_bn_beta", "L0_conv_bn_mean", "L0_conv_bn_var", "L0_conv_qk_w",
        "L0_conv_v_w", "L1_conv_w_out", "L1_conv_b_out"]


def kernel(**inputs):
    import numpy as _np
    import concourse.bacc as _bacc
    from concourse import mybir as _mybir
    from concourse.bass_utils import run_bass_kernel_spmd as _run

    nc = _bacc.Bacc("TRN2", target_bir_lowering=False, num_devices=1)
    arrays, args = {}, []
    for name in _INS:
        a = _np.ascontiguousarray(inputs[name])
        arrays[f"in_{name}_dram"] = a
        args.append(nc.dram_tensor(f"in_{name}_dram", a.shape, _mybir.dt.from_np(a.dtype), kind="ExternalInput").ap())
    args.append(nc.dram_tensor("out_dram", (B, C, H, W), _mybir.dt.float32, kind="ExternalOutput").ap())
    build(nc, *args)
    r = _run(nc, [arrays], core_ids=[0])
    return r.results[0]["out_dram"]
```

```python
from contextlib import ExitStack

import concourse.bass as bass
from concourse import mybir

F32 = mybir.dt.float32
ALU = mybir.AluOpType
ACT = mybir.ActivationFunctionType
AX_X = mybir.AxisListType.X

P = 128
B, C, H, W = 16, 64, 56, 56
HW = H * W
BP = B // 2
BANK = 512

WS = 7
NI = H // WS
S = WS * WS
SP = 64
ELT = 4 * S
UT = 2 * ELT
HEADS_R = 8
UNITS = BP * NI
VW = 48
ATT_SCALE = 16 ** -0.5
BN_EPS = 1e-6
GN_EPS = 1e-5

KS = 5
R = 2
RG = 8
GR = H // RG
HR = GR + 2 * R
WP = W + 2 * R
HALO = HR * WP
RAW = HR * W
PIX = GR * W
LH = 8
HD = C // LH
NK = KS * KS
CH = HD // 2
TILE = CH * (GR + R) * (W + R)
HALF_PLANE = [(0, 0), (0, 1), (0, 2)] + [(dy, dx) for dy in (1, 2) for dx in range(-2, 3)]
ALL_SHIFTS = [(dy, dx) for dy in range(-2, 3) for dx in range(-2, 3)]


def slot_of(dy, dx):
    return (dy + R) * KS + dx + R


def region(dy, dx):
    rows = GR + dy
    c0 = min(R, R - dx)
    return R - dy, rows, c0, W + abs(dx)


def segments(rows, cols):
    if rows * cols <= BANK:
        return [(0, rows)]
    half = (rows + 1) // 2
    return [(0, half), (half, rows)]


DVE_SLOTS, POOL_SLOTS = 2, 2
S_TILES = len(HALF_PLANE)
MAX_PARTS, SUB_PARTS = 4, KS
RATES = {"dve": (1.04, 80.0), "pool": (2.15, 150.0)}
GROUP = 4
SCORES_FROM, SCORES_TO = 4e3, 90e3


def plan(scores, values):
    s = [("s", t, a) for t in range(S_TILES) for a in range(2)] if scores else []
    v = [list(range(NK)), list(range(NK))] if values else [[], []]
    at, order, n_s = {"dve": 0.0, "pool": 0.0}, [], len(s)
    softmax = 2 * MAX_PARTS + SUB_PARTS + 1 if scores else 0
    while s or v[0] or v[1]:
        who = "dve" if at["dve"] <= at["pool"] else "pool"
        rate, fixed = RATES[who]
        half = 0 if v[0] else 1
        due = (n_s - len(s)) * (SCORES_TO - SCORES_FROM) < n_s * (at[who] - SCORES_FROM)
        if s and (due or not v[half]):
            _, t, a = s.pop(0)
            _, rows, _, cols = region(*HALF_PLANE[t])
            cost = CH * rows * cols * rate + fixed
            if who == "dve":
                cost += CH * rows * cols * rate / 2 + fixed
            task = ("s", t, a, who == "dve")
        else:
            n = GROUP if who == "dve" else 1
            ks, v[half] = tuple(v[half][:n]), v[half][n:]
            cost = (2 * len(ks) - 1) * (CH * PIX * rate + fixed)
            task = ("v", half, ks)
        at[who] += cost
        order.append([at[who], who, task])
        if who == "dve" and not s and softmax:
            at["dve"] += 2.4e3
            softmax -= 1
    first_half = max([o[0] for o in order if o[2][:2] == ("v", 0)], default=0)
    latest = 0
    for o in sorted(order, key=lambda o: o[2][1:3] if o[2][0] == "s" else (99, o[2][1])):
        if o[2][0] == "s":
            o[0] = latest = max(latest, o[0])
        elif o[2][1] == 1:
            o[0] = max(o[0], first_half + 1)
    order.sort(key=lambda o: o[0])
    return [(who, task) for _, who, task in order]


FULL, ONLY_S, ONLY_V = plan(True, True), plan(True, False), plan(False, True)


def count(tiles, who):
    return sum(1 for w, _ in tiles if w == who)


def links(tiles):
    return sum((1 if t[0] == "s" else 2 * len(t[2]) - 2) for w, t in tiles if w == "dve")


assert count(FULL, "dve") % DVE_SLOTS == 0 and count(FULL, "pool") % POOL_SLOTS == 0


def before(j, number):
    if isinstance(j, int) and j == 0:
        return 0
    return (j - 1) * number(FULL) + number(ONLY_S)


def tiles_before(j, who):
    return before(j, lambda tiles: count(tiles, who))


def slot(j, n, who, slots):
    first = 0 if isinstance(j, int) and j == 0 else count(ONLY_S, who)
    return (first + n) % slots


def build(nc, x, bn_gamma, bn_beta, bn_mean, bn_var, qk_w, v_w, w_out, b_out, out):
    x1_flat = nc.dram_tensor("x1_dram", (1, 2 * C * BP * HW + 2 * R * W), F32).ap()
    x1_dram = x1_flat[0:1, R * W:R * W + 2 * C * BP * HW].rearrange("o (p bp n) -> p (o bp) n", p=2 * C, bp=BP)
    attn_dram = nc.dram_tensor("attn_dram", (2, C, BP, RG, PIX), F32).ap()
    x_rows = x.rearrange("(bp b2) c h w -> (b2 c) bp (h w)", b2=2)
    out_rows = out.rearrange("(bp b2) c h w -> (b2 c) bp (h w)", b2=2)
    attn_rows = attn_dram.rearrange("b2 c bp rg n -> (b2 c) bp (rg n)")

    with ExitStack() as ctx:
        def sem(name):
            return ctx.enter_context(nc.semaphore(name))

        consts = ctx.enter_context(nc.sbuf_tensor("consts", [P, 2400], F32))
        arena = ctx.enter_context(nc.sbuf_tensor("arena", [P, 50400], F32))
        PS = ctx.enter_context(nc.psum_tensor("PS", [P, 8, BANK], F32))

        used = [0, 0]

        def const(n):
            used[0] += n
            assert used[0] <= 2400
            return consts[:, used[0] - n:used[0]]

        def room(n):
            used[1] += n
            assert used[1] <= 50400, used[1]
            return arena[:, used[1] - n:used[1]]

        ident = const(P)
        pair_mean = const(P)
        head_mask = const(HEADS_R)
        w_nat = [const(P) for _ in range(4)]
        w_T_all = const(4 * P)
        w_T = [w_T_all[:, n * P:(n + 1) * P] for n in range(4)]
        wqk_T, wv_T, wout_T = w_T[0:2], w_T[2], w_T[3]
        par = const(5)
        bn_inv, bn_off = const(1), const(1)
        chunk_stats = const(UNITS * 6)
        mean_var = const(BP * 2).rearrange("p (b s) -> p b s", s=2)
        g_mean, g_dev, g_std = const(BP), const(BP), const(BP)
        g_pair = const(2 * BP)
        g_rstd, g_bias = g_pair[:, 0:BP], g_pair[:, BP:2 * BP]
        row_sel = const(2 * 64)
        edge_ones = const(2 * 16)
        edge = const(2)
        pair_T = const(P)
        row_par = const(2 * C)
        no_rows = const(R * W)
        t_scale, t_bias, t_tmp = const(BP), const(BP), const(BP)

        xs = room(BP * HW).rearrange("p (b n) -> p b n", b=BP)
        tok = [room(UT) for _ in range(2)]
        qk_sb = [[room(UT + SP) for _ in range(2)] for _ in range(2)]
        v_ch = [room(2 * 4 * SP).rearrange("p (e r s) -> p e r s", e=2, r=4) for _ in range(2)]
        k_bd = [room(2 * HEADS_R * S).rearrange("p (r h s) -> p r h s", r=2, h=HEADS_R) for _ in range(4)]
        v_bd = [[room(16 * VW).rearrange("p (g n) -> p g n", n=VW) for _ in range(2)] for _ in range(2)]
        probs = [room(HEADS_R * SP).rearrange("p (h s) -> p h s", s=SP) for _ in range(4)]
        row_max = [room(HEADS_R) for _ in range(2)]
        probs_T = [room(4 * P).rearrange("p (j n) -> p j n", j=4) for _ in range(2)]
        rden = [room(HEADS_R) for _ in range(2)]
        o_tok = [room(2 * 2 * 2 * C).rearrange("p (e u b c) -> p e u b c", b=2, e=2, u=2) for _ in range(2)]
        res = [room(UT) for _ in range(2)]
        window_end = used[1]
        assert used[1] <= 50400

        used[1] = 0
        raw = [room(CH * RAW).rearrange("p (c n) -> p c n", c=CH) for _ in range(2)]
        xh = [room(HD * HALO).rearrange("p (c h w) -> p c h w", c=HD, h=HR) for _ in range(2)]
        sc = [room(NK * PIX).rearrange("p (k n) -> p k n", k=NK) for _ in range(2)]
        dve_ring = [room(TILE) for _ in range(DVE_SLOTS)]
        dve_extra = [room(CH * PIX) for _ in range(2)]
        pool_ring = [room(TILE) for _ in range(POOL_SLOTS)]
        smax = room(PIX)
        lsum = room(PIX)
        lden = [room(PIX) for _ in range(2)]
        o_loc = room(CH * PIX).rearrange("p (c n) -> p c n", c=CH)
        used[1] = 0
        x1_in = [room(HW) for _ in range(3)]
        at_in = [room(HW) for _ in range(3)]
        fin = [room(HW) for _ in range(2)]

        x_loaded = [sem(f"x_loaded{i}") for i in range(BP)]
        par_loaded = sem("par_loaded")
        w_zeroed = sem("w_zeroed")
        masks_ready = sem("masks_ready")
        bufs_zeroed = sem("bufs_zeroed")
        w_transposed = sem("w_transposed")
        wT_ready = sem("wT_ready")
        st = sem("st")
        gn_in = sem("gn_in")
        gn_out = sem("gn_out")
        sq_in = sem("sq_in")
        sq_out = sem("sq_out")
        affine_ready = sem("affine_ready")
        tok_ready = sem("tok_ready")
        proj_done = sem("proj_done")
        proj_copied = sem("proj_copied")
        kbd_ready = sem("kbd_ready")
        vtr_done = sem("vtr_done")
        vbd_ready = sem("vbd_ready")
        s_done = sem("s_done")
        max_done = sem("max_done")
        sub_done = sem("sub_done")
        exp_done = sem("exp_done")
        pt_done = sem("pt_done")
        pt_copied = sem("pt_copied")
        pv_done = sem("pv_done")
        rden_done = sem("rden_done")
        norm_done = sem("norm_done")
        ot_done = sem("ot_done")
        x1_stats = sem("x1_stats")
        res_ready = sem("res_ready")
        added = sem("added")
        pair_ready = sem("pair_ready")
        sel_done = sem("sel_done")
        row_par_ready = sem("row_par_ready")
        no_rows_ready = sem("no_rows_ready")
        edges_stored = sem("edges_stored")
        pads_zeroed = sem("pads_zeroed")
        x1_stored = sem("x1_stored")
        raw_loaded = [sem("raw_loaded0"), sem("raw_loaded1")]
        scaled = sem("scaled")
        xh_ready = sem("xh_ready")
        dprod = sem("dprod")
        dprod_used = sem("dprod_used")
        pprod = sem("pprod")
        pprod_used = sem("pprod_used")
        dlink = sem("dlink")
        sc_copied = sem("sc_copied")
        lmax_done = sem("lmax_done")
        lsub_done = sem("lsub_done")
        lexp_done = sem("lexp_done")
        lden_done = sem("lden_done")
        lsum_done = sem("lsum_done")
        out_norm = sem("out_norm")
        o_stored = sem("o_stored")
        fin_loaded = [sem(f"fin_loaded{i}") for i in range(3)]
        fproj = sem("fproj")
        fin_ready = sem("fin_ready")
        out_stored = [sem("out_stored0"), sem("out_stored1")]

        block = ctx.enter_context(nc.Block())

        def unit_pixels(u):
            off = (u // NI) * HW + (u % NI) * W
            first = arena[:, off:off + 1] if isinstance(u, int) else arena[:, bass.ds(off, 1)]
            return bass.AP(first.tensor, first.offset, [list(first.ap[0]), [1, NI], [NI * W, WS], [NI, WS]])

        def of_pair(t, u):
            return t[:, u // NI:u // NI + 1] if isinstance(u, int) else t[:, bass.ds(u // NI, 1)]

        def residue(buf, e, r):
            return buf[:, e * ELT + r:e * ELT + r + 4 * (SP - 1) + 1:4]

        def units(eng, unit, peel=1):
            for u in range(peel):
                unit(u, u % 2, u == 0, False)
            with eng.Fori(0, (UNITS - 1 - peel) // 2) as i:
                unit(peel + 2 * i, peel % 2, False, False)
                unit(peel + 1 + 2 * i, 1 - peel % 2, False, False)
            for u in range(peel + (UNITS - 1 - peel) // 2 * 2, UNITS):
                unit(u, u % 2, False, u == UNITS - 1)

        def heads(eng, iteration, looped=LH - 2):
            iteration(0, 0, True, False, ONLY_S)
            iteration(1, 1, True, True, FULL)
            with eng.Fori(0, looped // 2) as i:
                iteration(2 + 2 * i, 0, True, True, FULL)
                iteration(3 + 2 * i, 1, True, True, FULL)
            for j in range(2 + looped, LH):
                iteration(j, j % 2, True, True, FULL)
            iteration(LH, 0, False, True, ONLY_V)

        def multiply(eng, task, jp, buf):
            if task[0] == "s":
                _, t, a, _ = task
                dy, dx = HALF_PLANE[t]
                r0, rows, c0, cols = region(dy, dx)
                X = xh[jp][:, a * CH:(a + 1) * CH]
                tile = buf[:, 0:CH * rows * cols].rearrange("p (c h w) -> p c h w", c=CH, h=rows)
                return [(tile, X[:, :, r0:r0 + rows, c0:c0 + cols],
                         X[:, :, r0 + dy:r0 + dy + rows, c0 + dx:c0 + dx + cols])]
            _, half, ks = task
            X = xh[1 - jp][:, half * CH:(half + 1) * CH]
            ops = []
            for m, k in enumerate(ks):
                dst = dve_extra[m % 2] if m else buf[:, 0:CH * PIX]
                dy, dx = ALL_SHIFTS[k]
                weight = sc[1 - jp][:, k, :].rearrange("p (h w) -> p h w", w=W)
                ops.append((dst.rearrange("p (c h w) -> p c h w", c=CH, h=GR),
                            X[:, :, R + dy:R + dy + GR, R + dx:R + dx + W],
                            weight.unsqueeze(1).to_broadcast([P, CH, GR, W])))
            return ops

        def await_sums(eng, j, tiles, match):
            last = max(n for n, (_, t) in enumerate(tiles) if match(t))
            who = tiles[last][0]
            eng.wait_ge(dprod_used if who == "dve" else pprod_used,
                        tiles_before(j, who) + count(tiles[:last + 1], who))

        def await_pixels(eng, j, a):
            eng.wait_ge(xh_ready, 2 * j + a + 1)

        @block.sync
        def _(sp):
            for bp in range(BP):
                sp.dma_start(xs[:, bp, :], x_rows[:, bp, :]).then_inc(x_loaded[bp], 16)
            sp.wait_ge(w_zeroed, 1)
            for b2 in range(2):
                rows = slice(b2 * C, (b2 + 1) * C)
                sp.dma_start(w_nat[b2][:, rows], qk_w).then_inc(par_loaded, 16)
                sp.dma_start(w_nat[2][rows, rows], v_w).then_inc(par_loaded, 16)
                sp.dma_start(w_nat[3][rows, rows], w_out).then_inc(par_loaded, 16)
                for n, v in enumerate((bn_gamma, bn_beta, bn_mean, bn_var, b_out)):
                    sp.dma_start(par[rows, n:n + 1], v.rearrange("(c o) -> c o", o=1)).then_inc(par_loaded, 16)

            sp.wait_ge(no_rows_ready, 1)
            sp.dma_start(x1_flat[0:1, 0:R * W], no_rows[0:1, :]).then_inc(edges_stored, 16)
            sp.dma_start(x1_flat[0:1, R * W + 2 * C * BP * HW:], no_rows[0:1, :]).then_inc(edges_stored, 16)
            for bp in range(BP):
                sp.wait_ge(added, NI * (bp + 1))
                sp.dma_start(x1_dram[:, bp, :], xs[:, bp, :]).then_inc(x1_stored, 16)
            sp.wait_ge(x1_stored, 16 * BP)
            sp.wait_ge(edges_stored, 32)

            def load_half(j, a):
                for b2 in range(2):
                    off = b2 * C * BP * HW + (j * HD + a * CH) * BP * HW
                    at = x1_flat[0:1, off:off + 1] if isinstance(j, int) else x1_flat[0:1, bass.ds(off, 1)]
                    src = bass.AP(at.tensor, at.offset, [[PIX, C], [BP * HW, CH], [1, RAW]])
                    sp.dma_start(raw[a][b2 * C:(b2 + 1) * C], src).then_inc(raw_loaded[a], 16)

            def store_half(j, a):
                for b2 in range(2):
                    c0 = j * HD + a * CH
                    dst = attn_dram[b2, c0:c0 + CH] if isinstance(j, int) else attn_dram[b2, bass.ds(c0, CH)]
                    sp.dma_start(dst.rearrange("c bp rg n -> (bp rg) c n"),
                                 o_loc[b2 * C:(b2 + 1) * C]).then_inc(o_stored, 16)

            for j in range(2):
                for a in range(2):
                    if j:
                        sp.wait_ge(xh_ready, a + 1)
                    load_half(j, a)

            def iteration(j, jp, do_s, do_v, tiles):
                for a in range(2):
                    if do_v:
                        sp.wait_ge(out_norm, 2 * (j - 1) + a + 1)
                        store_half(j - 1, a)
                    if not isinstance(j, int) or j + 2 < LH:
                        sp.wait_ge(xh_ready, 2 * (j + 1) + a + 1)
                        load_half(j + 2, a)
            heads(sp, iteration, LH - 4)
            sp.wait_ge(o_stored, 16 * 4 * LH)

            def load_pair(bp):
                sp.dma_start(at_in[bp % 3], attn_rows[:, bp, :]).then_inc(fin_loaded[bp % 3], 16)
                sp.dma_start(x1_in[bp % 3], x1_dram[:, bp, :]).then_inc(fin_loaded[bp % 3], 16)
            for bp in range(3):
                load_pair(bp)
            for bp in range(BP):
                sp.wait_ge(fin_ready, 2 * bp + 2)
                sp.dma_start(out_rows[:, bp, :], fin[bp % 2]).then_inc(out_stored[bp % 2], 16)
                if bp + 3 < BP:
                    load_pair(bp + 3)
            for q in out_stored:
                sp.wait_ge(q, 16 * BP // 2)

        @block.gpsimd
        def _(pool):
            for w in w_nat:
                i = nc.gpsimd.memset(w, 0.0)
            i.then_inc(w_zeroed, 1)
            nc.gpsimd.memset(ident, 0.0)
            nc.gpsimd.memset(pair_mean, 0.5)
            nc.gpsimd.memset(row_sel, 1.0)
            nc.gpsimd.memset(edge_ones, 1.0)
            nc.gpsimd.memset(no_rows, 0.0).then_inc(no_rows_ready, 1)
            nc.gpsimd.memset(head_mask, 1.0).then_inc(masks_ready, 1)
            pool.wait_ge(masks_ready, 1)
            nc.gpsimd.affine_select(out=ident, in_=ident, compare_op=ALU.not_equal, fill=1.0, base=0,
                                    pattern=[[-1, P]], channel_multiplier=1)
            groups = pair_mean.rearrange("p (j k) -> p j k", k=2)
            nc.gpsimd.affine_select(out=groups, in_=groups, compare_op=ALU.is_ge, fill=0.0, base=0,
                                    pattern=[[-2, C], [0, 2]], channel_multiplier=1)
            for n in range(2):
                nc.gpsimd.affine_select(out=row_sel[:, n * C:(n + 1) * C], in_=row_sel[:, n * C:(n + 1) * C],
                                        compare_op=ALU.is_ge, fill=0.0, base=RG * BP * n, pattern=[[1, C]],
                                        channel_multiplier=-RG)
                nc.gpsimd.affine_select(out=edge_ones[:, n * 16:(n + 1) * 16], in_=edge_ones[:, n * 16:(n + 1) * 16],
                                        compare_op=ALU.not_equal, fill=0.0, base=-(RG - 1) * n,
                                        pattern=[[-RG, 16]], channel_multiplier=1)
            slots = head_mask.rearrange("p (j h) -> p j h", h=2)
            nc.gpsimd.affine_select(out=slots, in_=slots, compare_op=ALU.is_ge, fill=0.0, base=0,
                                    pattern=[[-16, 4], [-64, 2]], channel_multiplier=1).then_inc(masks_ready, 1)
            pool.wait_ge(masks_ready, 2)
            for n in range(2):
                nc.gpsimd.affine_select(out=row_sel[:, n * C:(n + 1) * C], in_=row_sel[:, n * C:(n + 1) * C],
                                        compare_op=ALU.is_ge, fill=0.0, base=RG - 1 - RG * BP * n, pattern=[[-1, C]],
                                        channel_multiplier=RG)
            nc.gpsimd.affine_select(out=groups, in_=groups, compare_op=ALU.is_ge, fill=0.0, base=1,
                                    pattern=[[2, C], [0, 2]], channel_multiplier=-1)
            nc.gpsimd.affine_select(out=slots, in_=slots, compare_op=ALU.is_ge, fill=0.0, base=15,
                                    pattern=[[16, 4], [64, 2]], channel_multiplier=-1).then_inc(masks_ready, 1)
            pool.wait_ge(masks_ready, 3)
            for u in range(2):
                for b2 in range(2):
                    nc.gpsimd.memset(qk_sb[u][b2][:, UT:UT + SP], 0.0)
                    nc.gpsimd.memset(v_bd[u][b2], 0.0)
                nc.gpsimd.memset(v_ch[u], 0.0)
            for q in probs:
                i = nc.gpsimd.memset(q, 0.0)
            i.then_inc(bufs_zeroed, 1)
            pool.wait_ge(bufs_zeroed, 1)
            for u in range(2):
                for e in range(2):
                    nc.gpsimd.memset(v_bd[u][e][0:SP, :, 32:33], 1.0)
                    i = nc.gpsimd.memset(v_bd[u][e][SP:P, :, 33:34], 1.0)
            i.then_inc(bufs_zeroed, 1)

            def expand_keys(k, up):
                b2, e = k // 2, k % 2
                for r in range(2):
                    keys = residue(qk_sb[up][b2], e, 2 + r)[:, 0:S]
                    i = nc.gpsimd.tensor_tensor(k_bd[k][:, r], keys.unsqueeze(1).to_broadcast([P, HEADS_R, S]),
                                                head_mask.unsqueeze(2).to_broadcast([P, HEADS_R, S]), ALU.mult)
                i.then_inc(kbd_ready, 1)

            def add_residual(u, up):
                pool.wait_ge(res_ready, 2 * u + 2)
                v = unit_pixels(u)
                nc.gpsimd.tensor_tensor(v, v, res[up].rearrange("p (i a c) -> p i a c", i=NI, a=WS),
                                        ALU.add).then_inc(added, 1)

            def unit(u, up, first, last):
                for k in range(4):
                    if k % 2 == 0:
                        pool.wait_ge(proj_copied, 3 * u + k // 2 + 1)
                    if not first:
                        pool.wait_ge(s_done, 4 * u + k - 3)
                    expand_keys(k, up)
                    if k == 1 and not (isinstance(u, int) and u < 2):
                        add_residual(u - 2, up)
            units(pool, unit, peel=2)
            add_residual(UNITS - 2, 0)
            add_residual(UNITS - 1, 1)

            pool.wait_ge(x1_stored, 16 * BP)
            for q in xh:
                nc.gpsimd.memset(q[:, :, :, 0:R], 0.0)
                i = nc.gpsimd.memset(q[:, :, :, R + W:WP], 0.0)
            i.then_inc(pads_zeroed, 1)
            pool.wait_ge(pads_zeroed, 1)

            def iteration(j, jp, do_s, do_v, tiles):
                n, done = 0, tiles_before(j, "pool")
                seen = set()
                if do_v:
                    pool.wait_ge(lexp_done, SUB_PARTS * j)
                for who, task in tiles:
                    if who != "pool":
                        continue
                    if task[0] == "s" and task[2] not in seen:
                        seen.add(task[2])
                        await_pixels(pool, j, task[2])
                    if not (isinstance(j, int) and j == 0 and n < POOL_SLOTS):
                        pool.wait_ge(pprod_used, done + n + 1 - POOL_SLOTS)
                    (o, a, b), = multiply(pool, task, jp, pool_ring[slot(j, n, "pool", POOL_SLOTS)])
                    nc.gpsimd.tensor_tensor(o, a, b, ALU.mult).then_inc(pprod, 1)
                    n += 1
            heads(pool, iteration)

        @block.scalar
        def _(act):
            act.wait_ge(wT_ready, 1)
            nc.scalar.activation(bn_inv, bn_off, ACT.Sqrt).then_inc(sq_out, 1)
            act.wait_ge(sq_in, 1)
            nc.scalar.activation(g_dev, g_std, ACT.Sqrt).then_inc(sq_out, 1)
            act.wait_ge(affine_ready, 1)
            act.wait_ge(bufs_zeroed, 2)

            def gather(u, up):
                nc.scalar.activation(tok[up].rearrange("p (i a c) -> p i a c", i=NI, a=WS), unit_pixels(u),
                                     ACT.Identity, bias=of_pair(t_bias, u), scale=of_pair(t_scale, u)
                                     ).then_inc(tok_ready, 1)

            def copy_qk(u, up, b2):
                act.wait_ge(proj_done, 3 * u + b2 + 1)
                nc.scalar.activation(qk_sb[up][b2][:, 0:UT], PS[:, 0, 0:UT], ACT.Copy).then_inc(proj_copied, 1)

            def copy_v(u, up):
                act.wait_ge(proj_done, 3 * u + 3)
                nc.scalar.activation(v_ch[up][:, :, :, 0:S], PS[:, 0, 0:UT].rearrange("p (e s r) -> p e r s", e=2, r=4),
                                     ACT.Relu).then_inc(proj_copied, 1)

            def place_values(u, up, e):
                act.wait_ge(vtr_done, 2 * u + e + 1)
                groups = PS[:, 1, 0:2 * P].rearrange("p (g n) -> p g n", n=16)
                for h in range(2):
                    rows = slice(h * SP, h * SP + S)
                    i = nc.scalar.activation(v_bd[up][e][rows, :, h * 16:h * 16 + 16], groups[rows], ACT.Copy)
                i.then_inc(vbd_ready, 1)

            def exponentials(n, k):
                act.wait_ge(sub_done, n + 1)
                nc.scalar.activation(probs[k][:, :, 0:S], probs[k][:, :, 0:S], ACT.Exp,
                                     scale=ATT_SCALE).then_inc(exp_done, 1)

            def copy_transposed(n, k, ready=True):
                act.wait_ge(pt_done, n + 1)
                if not (isinstance(n, int) and n < 2):
                    act.wait_ge(pv_done, n - 1)
                nc.scalar.activation(probs_T[k % 2].rearrange("p j n -> p (j n)"), PS[:, 4 + k % 2, :],
                                     ACT.Copy).then_inc(pt_copied, 1)

            gather(0, 0)
            for b2 in range(2):
                copy_qk(0, 0, b2)
            copy_v(0, 0)

            def unit(u, up, first, last):
                for k in range(4):
                    n = 4 * u + k
                    if not (first and k == 0):
                        copy_transposed(n - 1, (k - 1) % 4)
                    exponentials(n, k)
                    if k < 2:
                        place_values(u, up, k)
                    if not last:
                        if k == 0:
                            gather(u + 1, 1 - up)
                        elif k < 3:
                            copy_qk(u + 1, 1 - up, k - 1)
                        else:
                            copy_v(u + 1, 1 - up)
            units(act, unit)
            copy_transposed(4 * UNITS - 1, 3)

            act.wait_ge(sq_in, 2)
            nc.scalar.activation(g_dev, g_std, ACT.Sqrt).then_inc(sq_out, 1)
            act.wait_ge(row_par_ready, 1)

            def param(n, c):
                return row_par[:, n * C + c:n * C + c + 1] if isinstance(c, int) else \
                    row_par[:, bass.ds(n * C + c, 1)]

            def normalise_half(j, jp, a):
                act.wait_ge(raw_loaded[a], 32 * (j + 1))
                for c in range(CH):
                    chan = j * HD + a * CH + c
                    i = nc.scalar.activation(xh[jp][:, a * CH + c, :, R:R + W],
                                             raw[a][:, c, :].rearrange("p (h w) -> p h w", w=W),
                                             ACT.Identity, bias=param(1, chan), scale=param(0, chan))
                i.then_inc(scaled, 1)
                act.wait_ge(scaled, 2 * j + a + 1)
                for n, h in enumerate((0, R + GR)):
                    rows = xh[jp][:, a * CH:(a + 1) * CH, h:h + R, R:R + W]
                    i = nc.scalar.activation(rows, rows, ACT.Copy, scale=edge[:, n:n + 1])
                i.then_inc(xh_ready, 1)

            def copy_scores(j, jp, t, tiles):
                await_sums(act, j, tiles, lambda task: task[:2] == ("s", t))
                dy, dx = HALF_PLANE[t]
                r0, rows, c0, cols = region(dy, dx)
                segs = segments(rows, cols)
                for sy, sx, py, px in {(dy, dx, 0, 0), (-dy, -dx, -dy, -dx)}:
                    top, left = R + py - r0, R + px - c0
                    dst = sc[jp][:, slot_of(sy, sx), :].rearrange("p (h w) -> p h w", w=W)
                    for s, (a, b) in enumerate(segs):
                        lo, hi = max(a, top), min(b, top + GR)
                        if lo >= hi:
                            continue
                        src = PS[:, 2 * (t % 2) + s, 0:(b - a) * cols].rearrange("p (h w) -> p h w", w=cols)
                        i = nc.scalar.activation(dst[:, lo - top:hi - top], src[:, lo - a:hi - a, left:left + W],
                                                 ACT.Copy)
                i.then_inc(sc_copied, 1)

            def iteration(j, jp, do_s, do_v, tiles):
                if not do_s:
                    return
                if isinstance(j, int) and j == 0:
                    for head in range(2):
                        for a in range(2):
                            normalise_half(head, head, a)
                else:
                    act.wait_ge(dprod, tiles_before(j, "dve"))
                    act.wait_ge(pprod, tiles_before(j, "pool"))
                for t in range(S_TILES):
                    copy_scores(j, jp, t, tiles)
                more = do_v and not (isinstance(j, int) and j + 1 >= LH)
                if more:
                    await_sums(act, j, tiles, lambda task: task[:2] == ("v", 0))
                    normalise_half(j + 1, 1 - jp, 0)
                for m in range(SUB_PARTS):
                    act.wait_ge(lsub_done, SUB_PARTS * j + m + 1)
                    v = sc[jp][:, m * KS:(m + 1) * KS, :].rearrange("p k n -> p (k n)")
                    nc.scalar.activation(v, v, ACT.Exp).then_inc(lexp_done, 1)
                if more:
                    await_sums(act, j, tiles, lambda task: task[:2] == ("v", 1))
                    normalise_half(j + 1, 1 - jp, 1)
            heads(act, iteration, LH - 4)

        @block.vector
        def _(dve):
            steps = [0]

            def step(i):
                steps[0] += 1
                i.then_inc(st, 1)
                dve.wait_ge(st, steps[0])

            def group_stats(turn, chunks):
                for bp in range(BP):
                    i = nc.vector.bn_aggr(mean_var[:, bp, :], chunk_stats[:, bp * chunks * 6:(bp + 1) * chunks * 6])
                step(i)
                nc.vector.tensor_copy(t_tmp, mean_var[:, :, 0]).then_inc(gn_in, 1)
                dve.wait_ge(gn_out, 2 * turn + 1)
                step(nc.vector.tensor_copy(g_mean, PS[:, 0, 0:BP]))
                step(nc.vector.tensor_tensor(g_dev, mean_var[:, :, 0], g_mean, ALU.subtract))
                step(nc.vector.tensor_tensor(g_std, g_dev, g_dev, ALU.mult))
                nc.vector.tensor_tensor(t_tmp, g_std, mean_var[:, :, 1], ALU.add).then_inc(gn_in, 1)
                dve.wait_ge(gn_out, 2 * turn + 2)
                nc.vector.tensor_scalar(g_std, PS[:, 0, 0:BP], GN_EPS, None, ALU.add).then_inc(sq_in, 1)
                dve.wait_ge(sq_out, turn + 2)
                step(nc.vector.reciprocal(g_rstd, g_dev))
                return nc.vector.scalar_tensor_tensor(out=g_bias, in0=g_mean, scalar=-1.0, in1=g_rstd,
                                                      op0=ALU.mult, op1=ALU.mult)

            dve.wait_ge(par_loaded, 16 * 16)
            dve.wait_ge(masks_ready, 3)
            nc.vector.tensor_scalar(bn_off, par[:, 3:4], BN_EPS, None, ALU.add).then_inc(wT_ready, 1)
            dve.wait_ge(w_transposed, 1)
            nc.vector.tensor_copy(w_T_all, PS[:, 1, :]).then_inc(wT_ready, 1)
            dve.wait_ge(sq_out, 1)
            step(nc.vector.reciprocal(bn_off, bn_inv))
            step(nc.vector.tensor_tensor(bn_inv, bn_off, par[:, 0:1], ALU.mult))
            step(nc.vector.tensor_tensor(t_tmp[:, 0:1], par[:, 2:3], bn_inv, ALU.mult))
            step(nc.vector.tensor_tensor(bn_off, par[:, 1:2], t_tmp[:, 0:1], ALU.subtract))
            for bp in range(BP):
                dve.wait_ge(x_loaded[bp], 16)
                for k in range(7):
                    n = 7 * bp + k
                    i = nc.vector.bn_stats(chunk_stats[:, 6 * n:6 * n + 6], xs[:, bp, k * 448:(k + 1) * 448])
            step(i)
            step(group_stats(0, 7))
            for n in range(2):
                nc.vector.tensor_reduce(edge[:, n:n + 1], edge_ones[:, n * 16:(n + 1) * 16], AX_X, ALU.min)
            nc.vector.tensor_scalar(t_scale, g_rstd, bn_inv, None, ALU.mult)
            nc.vector.tensor_scalar(t_bias, g_bias, bn_inv, bn_off, ALU.mult, ALU.add).then_inc(affine_ready, 1)
            dve.wait_ge(bufs_zeroed, 2)

            def subtract_max(n, k):
                bank = PS[:, 2 + k % 2, :].rearrange("p (h s) -> p h s", s=SP)[:, :, 0:S]
                dve.wait_ge(s_done, n + 1)
                nc.vector.tensor_reduce(row_max[k % 2], bank, AX_X, ALU.max).then_inc(max_done, 1)
                dve.wait_ge(max_done, n + 1)
                if not (isinstance(n, int) and n < 4):
                    dve.wait_ge(pt_done, n - 3)
                nc.vector.tensor_tensor(probs[k][:, :, 0:S], bank,
                                        row_max[k % 2].unsqueeze(2).to_broadcast([P, HEADS_R, S]),
                                        ALU.subtract).then_inc(sub_done, 1)

            def normalise(n, k, up):
                b2, e = k // 2, k % 2
                rd = rden[k % 2].rearrange("p (j q) -> p j q", q=2)
                o = PS[:, 6, 0:8 * VW].rearrange("p (j r n) -> p j r n", j=4, r=2)
                dve.wait_ge(pv_done, n + 1)
                nc.vector.reciprocal(rd, o[:, :, 0, 32:34]).then_inc(rden_done, 1)
                dve.wait_ge(rden_done, n + 1)
                for r in range(2):
                    rows = slice(r * SP, (r + 1) * SP)
                    dst = o_tok[up][rows, e, :, b2, :].rearrange("p q (j d) -> p j q d", j=4)
                    i = nc.vector.tensor_tensor(dst, o[rows, :, r, 0:32].rearrange("p j (q d) -> p j q d", q=2),
                                                rd[rows].unsqueeze(3).to_broadcast([SP, 4, 2, 16]), ALU.mult)
                i.then_inc(norm_done, 1)

            def order_tokens(u, up):
                dve.wait_ge(ot_done, u + 1)
                if not (isinstance(u, int) and u < 2):
                    dve.wait_ge(added, u - 1)
                for e in range(2):
                    src = PS[:, 7, e * 2 * P:(e + 1) * 2 * P].rearrange("p (h r s) -> p h r s", h=2, r=2)[:, :, :, 0:S]
                    dst = res[up][:, e * ELT:(e + 1) * ELT].rearrange("p (s r h) -> p h r s", r=2, h=2)
                    nc.vector.tensor_copy(dst, src).then_inc(res_ready, 1)

            def unit(u, up, first, last):
                for k in range(4):
                    n = 4 * u + k
                    subtract_max(n, k)
                    if not (first and k < 2):
                        normalise(n - 2, (k - 2) % 4, up if k >= 2 else 1 - up)
                    if k == 3 and not first:
                        order_tokens(u - 1, 1 - up)
                    if k == 3 and not (isinstance(u, int) and u < 3):
                        unit_stats(u - 3)

            def unit_stats(u):
                s = chunk_stats[:, 6 * u:6 * u + 6] if isinstance(u, int) else chunk_stats[:, bass.ds(6 * u, 6)]
                nc.vector.bn_stats(s, unit_pixels(u)).then_inc(x1_stats, 1)
            units(dve, unit, peel=3)
            normalise(4 * UNITS - 2, 2, 1)
            normalise(4 * UNITS - 1, 3, 1)
            order_tokens(UNITS - 1, 1)

            for u in range(UNITS - 3, UNITS):
                dve.wait_ge(added, u + 1)
                unit_stats(u)
            dve.wait_ge(x1_stats, UNITS)
            group_stats(1, NI).then_inc(pair_ready, 1)
            dve.wait_ge(sel_done, 1)
            nc.vector.tensor_copy(pair_T[0:2 * BP], PS[0:2 * BP, 1, 0:P]).then_inc(pair_ready, 1)
            dve.wait_ge(sel_done, 2)
            nc.vector.tensor_copy(row_par, PS[:, 2, 0:2 * C]).then_inc(row_par_ready, 1)
            dve.wait_ge(pads_zeroed, 1)

            def norm_half(j, jp, a, tiles):
                await_sums(dve, j, tiles, lambda task: task[:2] == ("v", a))
                if not (isinstance(j, int) and j == 1 and a == 0):
                    dve.wait_ge(o_stored, 64 * (j - 1) + 32 * a)
                nc.vector.tensor_tensor(o_loc, PS[:, 4:8, 0:PIX],
                                        lden[1 - jp].unsqueeze(1).to_broadcast([P, CH, PIX]),
                                        ALU.mult).then_inc(out_norm, 1)

            def softmax_steps(j, jp):
                w = PIX // MAX_PARTS
                for m in range(MAX_PARTS):
                    def step_max(m=m):
                        if m == 0:
                            dve.wait_ge(sc_copied, S_TILES * (j + 1))
                        nc.vector.tensor_reduce(smax[:, m * w:(m + 1) * w],
                                                sc[jp][:, :, m * w:(m + 1) * w].rearrange("p k n -> p n k"),
                                                AX_X, ALU.max).then_inc(lmax_done, 1)
                    yield step_max
                for m in range(SUB_PARTS):
                    def step_sub(m=m):
                        if m == 0:
                            dve.wait_ge(lmax_done, MAX_PARTS * (j + 1))
                        v = sc[jp][:, m * KS:(m + 1) * KS, :]
                        nc.vector.tensor_tensor(v, v, smax.unsqueeze(1).to_broadcast([P, KS, PIX]),
                                                ALU.subtract).then_inc(lsub_done, 1)
                    yield step_sub
                for m in range(MAX_PARTS):
                    def step_sum(m=m):
                        if m == 0:
                            dve.wait_ge(lexp_done, SUB_PARTS * (j + 1))
                        nc.vector.tensor_reduce(lsum[:, m * w:(m + 1) * w],
                                                sc[jp][:, :, m * w:(m + 1) * w].rearrange("p k n -> p n k"),
                                                AX_X, ALU.add).then_inc(lsum_done, 1)
                    yield step_sum

                def step_inverse():
                    dve.wait_ge(lsum_done, MAX_PARTS * (j + 1))
                    nc.vector.reciprocal(lden[jp], lsum).then_inc(lden_done, 1)
                yield step_inverse

            def iteration(j, jp, do_s, do_v, tiles):
                n, done = 0, tiles_before(j, "dve")
                linked = before(j, links)
                seen = set()
                soft = list(softmax_steps(j, jp)) if do_s else []
                last_s = max([i for i, (_, t) in enumerate(tiles) if t[0] == "s"], default=0)
                last_v0 = max([i for i, (_, t) in enumerate(tiles) if t[0] == "v" and t[1] == 0], default=0)
                if do_v:
                    dve.wait_ge(lden_done, j)
                for i, (who, task) in enumerate(tiles):
                    if do_v and i == last_v0 + 3:
                        norm_half(j, jp, 0, tiles)
                    if do_s and i > last_s + 1 and soft:
                        soft.pop(0)()
                    if who != "dve":
                        continue
                    if task[0] == "s" and task[2] not in seen:
                        seen.add(task[2])
                        await_pixels(dve, j, task[2])
                    if not (isinstance(j, int) and j == 0 and n < DVE_SLOTS):
                        dve.wait_ge(dprod_used, done + n + 1 - DVE_SLOTS)
                    buf = dve_ring[slot(j, n, "dve", DVE_SLOTS)]
                    ops = multiply(dve, task, jp, buf)
                    if task[0] == "s":
                        _, rows, _, cols = region(*HALF_PLANE[task[1]])
                        w = CH // 2 * rows * cols
                        nc.vector.tensor_tensor(*ops[0], ALU.mult).then_inc(dlink, 1)
                        linked += 1
                        dve.wait_ge(dlink, linked)
                        nc.vector.tensor_tensor(buf[:, 0:w], buf[:, 0:w], buf[:, w:2 * w], ALU.add).then_inc(dprod, 1)
                    elif len(ops) == 1:
                        nc.vector.tensor_tensor(*ops[0], ALU.mult).then_inc(dprod, 1)
                    else:
                        total = buf[:, 0:CH * PIX]
                        nc.vector.tensor_tensor(*ops[0], ALU.mult).then_inc(dlink, 1)
                        dve.wait_ge(dprod, done + n)
                        nc.vector.tensor_tensor(*ops[1], ALU.mult).then_inc(dlink, 1)
                        linked += 2
                        summed = linked
                        for m in range(1, len(ops)):
                            if m + 1 < len(ops):
                                if m > 1:
                                    dve.wait_ge(dlink, summed)
                                nc.vector.tensor_tensor(*ops[m + 1], ALU.mult).then_inc(dlink, 1)
                                linked += 1
                            dve.wait_ge(dlink, summed)
                            i = nc.vector.tensor_tensor(total, total, dve_extra[m % 2], ALU.add)
                            if m + 1 < len(ops):
                                i.then_inc(dlink, 1)
                                linked += 1
                                summed = linked
                            else:
                                i.then_inc(dprod, 1)
                    n += 1
                for s in soft:
                    s()
                if do_v:
                    norm_half(j, jp, 1, tiles)
            heads(dve, iteration)

            for bp in range(BP):
                dve.wait_ge(fin_loaded[bp % 3], 32 * (bp // 3 + 1))
                if bp >= 2:
                    dve.wait_ge(out_stored[bp % 2], 16 * (bp // 2))
                for g in range(2):
                    dve.wait_ge(fproj, 2 * bp + g + 1)
                    cols = slice(g * 4 * PIX, (g + 1) * 4 * PIX)
                    nc.vector.scalar_tensor_tensor(
                        out=fin[bp % 2][:, cols].rearrange("p (k n) -> p k n", k=4), in0=PS[:, 4 * g:4 * g + 4, 0:PIX],
                        scalar=par[:, 4:5], in1=x1_in[bp % 3][:, cols].rearrange("p (k n) -> p k n", k=4),
                        op0=ALU.add, op1=ALU.add).then_inc(fin_ready, 1)

        @block.tensor
        def _(pe):
            pe.wait_ge(masks_ready, 3)
            pe.wait_ge(par_loaded, 16 * 16)
            for n, w in enumerate(w_nat):
                i = nc.tensor.transpose(PS[:, 1, n * P:(n + 1) * P], w, ident)
            i.then_inc(w_transposed, 1)

            def pair_means(turn):
                for k in range(2):
                    pe.wait_ge(gn_in, 2 * turn + k + 1)
                    nc.tensor.matmul(PS[:, 0, 0:BP], pair_mean, t_tmp, start=True, stop=True).then_inc(gn_out, 1)

            pair_means(0)
            pe.wait_ge(wT_ready, 2)

            def project_qk(u, up, b2):
                if b2 == 0:
                    pe.wait_ge(tok_ready, u + 1)
                if not (isinstance(u, int) and u == 0 and b2 == 0):
                    pe.wait_ge(proj_copied, 3 * u + b2)
                nc.tensor.matmul(PS[:, 0, 0:UT], wqk_T[b2], tok[up], start=True, stop=True).then_inc(proj_done, 1)

            def project_v(u, up):
                pe.wait_ge(proj_copied, 3 * u + 2)
                nc.tensor.matmul(PS[:, 0, 0:UT], wv_T, tok[up], start=True, stop=True).then_inc(proj_done, 1)

            def transpose_v(u, up, e):
                pe.wait_ge(proj_copied, 3 * u + 3)
                if not (isinstance(u, int) and u == 0 and e == 0):
                    pe.wait_ge(vbd_ready, 2 * u + e)
                for r in range(2):
                    i = nc.tensor.transpose(PS[:, 1, r * P:(r + 1) * P],
                                            v_ch[up][:, e, 2 * r:2 * r + 2, :].rearrange("p r s -> p (r s)"), ident)
                i.then_inc(vtr_done, 1)

            def scores(n, k, up):
                b2, e = k // 2, k % 2
                pe.wait_ge(kbd_ready, n + 1)
                if not (isinstance(n, int) and n < 2):
                    pe.wait_ge(sub_done, n - 1)
                for r in range(2):
                    dst = PS[r * SP:(r + 1) * SP, 2 + k % 2, :].rearrange("p (h s) -> p h s", s=SP)[:, :, 0:S]
                    i = nc.tensor.matmul(dst, residue(qk_sb[up][b2], e, r), k_bd[k][:, r], start=True, stop=True)
                i.then_inc(s_done, 1)

            def transpose_probs(n, k):
                pe.wait_ge(exp_done, n + 1)
                if not (isinstance(n, int) and n < 2):
                    pe.wait_ge(pt_copied, n - 1)
                for j in range(4):
                    i = nc.tensor.transpose(PS[:, 4 + k % 2, j * P:(j + 1) * P],
                                            probs[k][:, 2 * j:2 * j + 2, :].rearrange("p h s -> p (h s)"), ident)
                i.then_inc(pt_done, 1)

            def weigh_values(n, k, up, vbd):
                b2, e = k // 2, k % 2
                pe.wait_ge(pt_copied, n + 1)
                pe.wait_ge(vbd_ready, vbd)
                if not (isinstance(n, int) and n == 0):
                    pe.wait_ge(norm_done, n)
                for j in range(4):
                    g = b2 * 4 + j
                    i = nc.tensor.matmul(PS[:, 6, 2 * VW * j:2 * VW * (j + 1)], probs_T[k % 2][:, j, :],
                                         v_bd[up][e][:, g:g + 9:8, :], start=True, stop=True)
                i.then_inc(pv_done, 1)

            def transpose_output(u, up):
                pe.wait_ge(norm_done, 4 * u + 4)
                if not (isinstance(u, int) and u == 0):
                    pe.wait_ge(res_ready, 2 * u)
                for e in range(2):
                    for h in range(2):
                        q = 2 * e + h
                        i = nc.tensor.transpose(PS[:, 7, q * P:(q + 1) * P], o_tok[up][:, e, h].rearrange("p b c -> p (b c)"), ident)
                i.then_inc(ot_done, 1)

            for b2 in range(2):
                project_qk(0, 0, b2)
            project_v(0, 0)

            def unit(u, up, first, last):
                for k in range(4):
                    n = 4 * u + k
                    scores(n, k, up)
                    if k < 2:
                        transpose_v(u, up, k)
                    if not (first and k == 0):
                        transpose_probs(n - 1, (k - 1) % 4)
                    if not (first and k < 2):
                        m = (k - 2) % 4
                        weigh_values(n - 2, m, up if k >= 2 else 1 - up,
                                     2 * u + m % 2 + 1 - (0 if k >= 2 else 2))
                    if not last:
                        if k in (1, 2):
                            project_qk(u + 1, 1 - up, k - 1)
                        elif k == 3:
                            project_v(u + 1, 1 - up)
                    if k == 3 and not first:
                        transpose_output(u - 1, 1 - up)
            units(pe, unit)
            transpose_probs(4 * UNITS - 1, 3)
            for k in (2, 3):
                weigh_values(4 * UNITS - 4 + k, k, 1, 2 * UNITS)
            transpose_output(UNITS - 1, 1)
            pair_means(1)
            pe.wait_ge(pair_ready, 1)
            nc.tensor.transpose(PS[0:2 * BP, 1, 0:P], g_pair, ident).then_inc(sel_done, 1)
            pe.wait_ge(pair_ready, 2)
            for n in range(2):
                for b2 in range(2):
                    i = nc.tensor.matmul(PS[b2 * C:(b2 + 1) * C, 2, n * C:(n + 1) * C], row_sel[0:2 * BP, n * C:(n + 1) * C],
                                         pair_T[0:2 * BP, b2 * C:(b2 + 1) * C], start=True, stop=True)
            i.then_inc(sel_done, 1)

            def iteration(j, jp, do_s, do_v, tiles):
                made = {"dve": tiles_before(j, "dve"), "pool": tiles_before(j, "pool")}
                n = {"dve": 0, "pool": 0}
                vs = [[t for _, t in tiles if t[0] == "v" and t[1] == a] for a in range(2)]
                for who, task in tiles:
                    ring, slots, ready, used_up = (dve_ring, DVE_SLOTS, dprod, dprod_used) if who == "dve" else \
                        (pool_ring, POOL_SLOTS, pprod, pprod_used)
                    buf = ring[slot(j, n[who], who, slots)]
                    n[who] += 1
                    pe.wait_ge(ready, made[who] + n[who])
                    if task[0] == "s":
                        _, t, a, folded = task
                        chans = CH // 2 if folded else CH
                        _, rows, _, cols = region(*HALF_PLANE[t])
                        if a == 0 and not (isinstance(j, int) and j == 0 and t < 2):
                            pe.wait_ge(sc_copied, S_TILES * j + t - 1)
                        for c in range(chans):
                            for s, (lo, hi) in enumerate(segments(rows, cols)):
                                i = nc.tensor.matmul(
                                    PS[:, 2 * (t % 2) + s, 0:(hi - lo) * cols], ident,
                                    buf[:, (c * rows + lo) * cols:(c * rows + hi) * cols],
                                    start=(a == 0 and c == 0), stop=(a == 1 and c == chans - 1))
                        i.then_inc(used_up, 1)
                    else:
                        _, half, ks = task
                        first, last = task == vs[half][0], task == vs[half][-1]
                        if first and not (isinstance(j, int) and j == 1 and half == 0):
                            pe.wait_ge(out_norm, 2 * (j - 1) + half)
                        for c in range(CH):
                            i = nc.tensor.matmul(PS[:, 4 + c, 0:PIX], ident, buf[:, c * PIX:(c + 1) * PIX],
                                                 start=first, stop=last)
                        i.then_inc(used_up, 1)
            heads(pe, iteration)

            for bp in range(BP):
                pe.wait_ge(fin_loaded[bp % 3], 32 * (bp // 3 + 1))
                for g in range(2):
                    if bp:
                        pe.wait_ge(fin_ready, 2 * bp + g - 1)
                    for k in range(4 * g, 4 * g + 4):
                        i = nc.tensor.matmul(PS[:, k, 0:PIX], wout_T, at_in[bp % 3][:, k * PIX:(k + 1) * PIX],
                                             start=True, stop=True)
                    i.then_inc(fproj, 1)


_INS = ["x", "L0_conv_bn_gamma", "L0_conv_bn_beta", "L0_conv_bn_mean", "L0_conv_bn_var", "L0_conv_qk_w",
        "L0_conv_v_w", "L1_conv_w_out", "L1_conv_b_out"]


def kernel(**inputs):
    import numpy as _np
    import concourse.bacc as _bacc
    from concourse import mybir as _mybir
    from concourse.bass_utils import run_bass_kernel_spmd as _run

    nc = _bacc.Bacc("TRN2", target_bir_lowering=False, num_devices=1)
    arrays, args = {}, []
    for name in _INS:
        a = _np.ascontiguousarray(inputs[name])
        arrays[f"in_{name}_dram"] = a
        args.append(nc.dram_tensor(f"in_{name}_dram", a.shape, _mybir.dt.from_np(a.dtype), kind="ExternalInput").ap())
    args.append(nc.dram_tensor("out_dram", (B, C, H, W), _mybir.dt.float32, kind="ExternalOutput").ap())
    build(nc, *args)
    r = _run(nc, [arrays], core_ids=[0])
    return r.results[0]["out_dram"]
```

```python
from contextlib import ExitStack

import concourse.bass as bass
from concourse import mybir

F32 = mybir.dt.float32
ALU = mybir.AluOpType
ACT = mybir.ActivationFunctionType
AX_X = mybir.AxisListType.X

P = 128
B, C, H, W = 16, 64, 56, 56
HW = H * W
BP = B // 2
BANK = 512

WS = 7
NI = H // WS
S = WS * WS
SP = 64
ELT = 4 * S
UT = 2 * ELT
HEADS_R = 8
UNITS = BP * NI
VW = 48
ATT_SCALE = 16 ** -0.5
BN_EPS = 1e-6
GN_EPS = 1e-5

CHUNKS = 7
STATS_UNIT = 6
STATS_OF = [range(CHUNKS + (BP - 1) * CHUNKS * q // (4 * STATS_UNIT), CHUNKS + (BP - 1) * CHUNKS * (q + 1) // (4 * STATS_UNIT))
            for q in range(4 * STATS_UNIT)]
PEEL = STATS_UNIT + 1
PAIRS_OF_TURN = [slice(0, 1), slice(1, BP), slice(0, BP)]

KS = 5
R = 2
RG = 8
GR = H // RG
HR = GR + 2 * R
WP = W + 2 * R
HALO = HR * WP
RAW = HR * W
PIX = GR * W
LH = 8
HD = C // LH
NK = KS * KS
CH = HD // 2
TILE = CH * (GR + R) * (W + R)
HALF_PLANE = [(0, 0), (0, 1), (0, 2)] + [(dy, dx) for dy in (1, 2) for dx in range(-2, 3)]
ALL_SHIFTS = [(dy, dx) for dy in range(-2, 3) for dx in range(-2, 3)]


def slot_of(dy, dx):
    return (dy + R) * KS + dx + R


def region(dy, dx):
    rows = GR + dy
    c0 = min(R, R - dx)
    return R - dy, rows, c0, W + abs(dx)


def segments(rows, cols):
    if rows * cols <= BANK:
        return [(0, rows)]
    half = (rows + 1) // 2
    return [(0, half), (half, rows)]


SLOTS = {"dve": 2, "pool": 3}
S_TILES = len(HALF_PLANE)
MAX_PARTS, SUB_PARTS = 4, KS
SOFT_STEPS = 2 * MAX_PARTS + SUB_PARTS + 1
RATES = {"dve": (1.04, 130.0), "pool": (2.15, 150.0), "pe": (1.67, 0.0), "act": (0.85, 250.0)}
SOFT_SAME = 4
GROUP = 4
SOFT_RUN = 1
SCORES_TO = 130e3
LATE_PIXELS = 6e3


def tile_columns(task):
    if task[0] == "s":
        _, rows, _, cols = region(*HALF_PLANE[task[1]])
        return CH * rows * cols
    return CH * PIX


def span(eng, columns, instructions=1):
    return columns * RATES[eng][0] + instructions * RATES[eng][1]


def plan(scores, values, soft_first=SOFT_STEPS, soft_last=0, norm_first=False, group=GROUP, scores_to=SCORES_TO,
         soft_run=SOFT_RUN):
    s = [("s", t, a) for t0 in range(0, S_TILES, 2) for a in range(2)
         for t in range(t0, min(t0 + 2, S_TILES))] if scores else []
    v = [list(range(NK)), list(range(NK))] if values else [[], []]
    n_s = len(s)
    free = {"dve": 0.0, "pool": 0.0, "pe": 0.0, "act": 0.0}
    used_up = {"dve": [], "pool": []}
    flying = []
    unsummed = [NK, NK]
    unscored = [2] * S_TILES
    copied = {}
    steps = []
    norms = [(1e3, (2, 1))] if norm_first else []
    softs = [(0.0, (1, m)) for m in range(soft_first, SOFT_STEPS)]
    exps = {"todo": min(SUB_PARTS, max(0, MAX_PARTS + SUB_PARTS - soft_first)), "end": 0.0, "run": 0}

    def act(ready, length, step):
        start = max(free["act"], ready)
        free["act"] = start + length
        steps.append((start, len(steps), step))
        return free["act"]

    def sum_until(time):
        while flying and min(flying)[0] <= time:
            end, who, task, columns = min(flying)
            flying.remove(min(flying))
            start = max(free["pe"], end)
            if task[0] == "s" and task[1] >= 2:
                start = max(start, copied[task[1] - 2])
            free["pe"] = start + span("pe", columns)
            used_up[who].append(free["pe"])
            steps.append((end, len(steps), (who, task)))
            if task[0] == "s":
                unscored[task[1]] -= 1
            if task[0] == "s" and not unscored[task[1]]:
                copied[task[1]] = act(free["pe"], 2 * span("act", PIX), ("copy", task[1]))
                if task[1] == S_TILES - 1:
                    softs.extend((copied[task[1]], (0, m)) for m in range(soft_last))
            if task[0] == "v":
                unsummed[task[1]] -= len(task[2])
                if not unsummed[task[1]]:
                    if task[1] == 0 or not scores:
                        norms.append((free["pe"], (1, task[1])))
                    if scores:
                        act(end, CH * span("act", RAW) + span("act", CH * PIX), ("pixels", task[1]))

    def vector_step(time, wait):
        if norms and (norms[0][0] <= time + 300 or wait):
            ready, step = norms.pop(0)
            start = max(time, ready)
            steps.append((start, len(steps), ("norm", step)))
            free["dve"] = start + span("dve", CH * PIX)
            return True
        if not softs or (exps["run"] >= soft_run and not wait):
            return False
        ready, (offset, m) = softs[0]
        if m >= MAX_PARTS + SUB_PARTS:
            ready = max(ready, exps["end"])
        if ready > time + 300 and not wait:
            return False
        softs.pop(0)
        exps["run"] += 1
        start = max(time, ready)
        steps.append((start, len(steps), ("soft", (offset, m))))
        sub = MAX_PARTS <= m < MAX_PARTS + SUB_PARTS
        free["dve"] = start + span("dve", KS * PIX if sub else 6 * PIX if m == SOFT_STEPS - 1 else NK * PIX // MAX_PARTS)
        if sub:
            exps["end"] = act(free["dve"], span("act", KS * PIX), ("exp", (offset, m - MAX_PARTS)))
            exps["todo"] -= offset
        return True

    while s or v[0] or v[1]:
        start = {}
        for w in ("dve", "pool"):
            n = len(used_up[w]) + sum(f[1] == w for f in flying)
            start[w] = free[w] if n < SLOTS[w] else \
                max(free[w], used_up[w][n - SLOTS[w]] if n - SLOTS[w] < len(used_up[w]) else float("inf"))
        who = "dve" if start["dve"] <= start["pool"] else "pool"
        time = start[who]
        if flying and min(flying)[0] <= time:
            sum_until(min(flying)[0])
            continue
        if who == "dve" and vector_step(time, False):
            continue
        half = 0 if v[0] else 1
        can_v = v[half] and exps["todo"] <= 0 and not any(n == (2, 1) for _, n in norms) and \
            (half == 0 or not (unsummed[0] or norms))
        can_s = s and (s[0][2] == 0 or time >= LATE_PIXELS or not norm_first)
        due = (n_s - len(s)) * scores_to < n_s * time
        if can_s and (due or not can_v):
            task = s.pop(0) + (who == "dve",)
            columns = tile_columns(task)
            length = span(who, columns)
            if who == "dve":
                columns //= 2
                length += span(who, columns)
        elif can_v:
            n = group if who == "dve" else 1
            task = ("v", half, tuple(v[half][:n]))
            v[half] = v[half][n:]
            columns = CH * PIX
            length = (2 * len(task[2]) - 1) * span(who, columns)
        else:
            if who == "dve" and not flying and vector_step(time, True):
                continue
            free[who] = time + 200
            continue
        if who == "dve":
            exps["run"] = 0
        free[who] = time + length
        flying.append((time + length, who, task, columns))
    sum_until(float("inf"))
    while vector_step(free["dve"], True):
        pass
    return [step for _, _, step in sorted(steps)]


ONLY_S = plan(True, False, soft_last=SOFT_SAME)
SECOND = plan(True, True, soft_first=SOFT_SAME, soft_last=SOFT_SAME, soft_run=2)
FULL = plan(True, True, soft_first=SOFT_SAME, soft_last=SOFT_SAME, norm_first=True)
LAST = plan(True, True, soft_first=SOFT_SAME, soft_last=SOFT_STEPS, norm_first=True, scores_to=67.5e3, group=2)
ONLY_V = plan(False, True, norm_first=True, group=3)
PLANS = [ONLY_S, SECOND] + [FULL] * (LH - 3) + [LAST, ONLY_V]


def count(steps, who):
    return sum(1 for w, _ in steps if w == who)


def copies_until(steps, t):
    copies = [task for kind, task in steps if kind == "copy"]
    return copies.index(t) + 1 if t >= 0 else 0


def links(steps):
    return sum((1 if t[0] == "s" else 2 * len(t[2]) - 2) for w, t in steps if w == "dve")


def before(j, number):
    if isinstance(j, int) and j < 2:
        return j * number(ONLY_S)
    if isinstance(j, int) and j == LH:
        return before(LH - 1, number) + number(LAST)
    return number(ONLY_S) + number(SECOND) + (j - 2) * number(FULL)


def tiles_before(j, who):
    return before(j, lambda steps: count(steps, who))


def slot_free(j, n, who):
    if n >= SLOTS[who]:
        return tiles_before(j, who) + n + 1 - SLOTS[who]
    if isinstance(j, int):
        earlier = [PLANS[j - 1]]
    else:
        earlier = [SECOND, FULL]
    return tiles_before(j, who) - min((count(steps, who) - 1 - n) % SLOTS[who] for steps in earlier)


def build(nc, x, bn_gamma, bn_beta, bn_mean, bn_var, qk_w, v_w, w_out, b_out, out):
    x1_flat = nc.dram_tensor("x1_dram", (1, 2 * C * BP * HW + 2 * R * W), F32).ap()
    x1_dram = x1_flat[0:1, R * W:R * W + 2 * C * BP * HW].rearrange("o (p bp n) -> p (o bp) n", p=2 * C, bp=BP)
    attn_dram = nc.dram_tensor("attn_dram", (2, C, BP, RG, PIX), F32).ap()
    x_rows = x.rearrange("(bp b2) c h w -> (b2 c) bp (h w)", b2=2)
    out_rows = out.rearrange("(bp b2) c h w -> (b2 c) bp (h w)", b2=2)
    attn_rows = attn_dram.rearrange("b2 c bp rg n -> (b2 c) bp (rg n)")

    with ExitStack() as ctx:
        def sem(name):
            return ctx.enter_context(nc.semaphore(name))

        consts = ctx.enter_context(nc.sbuf_tensor("consts", [P, 2400], F32))
        arena = ctx.enter_context(nc.sbuf_tensor("arena", [P, 50400], F32))
        PS = ctx.enter_context(nc.psum_tensor("PS", [P, 8, BANK], F32))

        used = [0, 0]

        def const(n):
            used[0] += n
            assert used[0] <= 2400
            return consts[:, used[0] - n:used[0]]

        def room(n):
            used[1] += n
            assert used[1] <= 50400, used[1]
            return arena[:, used[1] - n:used[1]]

        ident = const(P)
        pair_mean = const(P)
        head_mask = const(HEADS_R)
        w_nat = [const(P) for _ in range(4)]
        w_T_all = const(4 * P)
        w_T = [w_T_all[:, n * P:(n + 1) * P] for n in range(4)]
        wqk_T, wv_T, wout_T = w_T[0:2], w_T[2], w_T[3]
        par = const(5)
        bn_inv, bn_off = const(1), const(1)
        chunk_stats = const(UNITS * 6)
        mean_var = const(BP * 2).rearrange("p (b s) -> p b s", s=2)
        g_mean, g_dev, g_std = const(BP), const(BP), const(BP)
        g_pair = const(2 * BP)
        g_rstd, g_bias = g_pair[:, 0:BP], g_pair[:, BP:2 * BP]
        row_sel = const(2 * 64)
        edge_ones = const(2 * 16)
        edge = const(2)
        pair_T = const(P)
        row_par = const(2 * C)
        no_rows = const(R * W)
        t_scale, t_bias, t_tmp = const(BP), const(BP), const(BP)

        xs = room(BP * HW).rearrange("p (b n) -> p b n", b=BP)
        tok = [room(UT) for _ in range(2)]
        qk_sb = [[room(UT + SP) for _ in range(2)] for _ in range(2)]
        v_ch = [room(2 * 4 * SP).rearrange("p (e r s) -> p e r s", e=2, r=4) for _ in range(2)]
        k_bd = [room(2 * HEADS_R * S).rearrange("p (r h s) -> p r h s", r=2, h=HEADS_R) for _ in range(4)]
        v_bd = [[room(16 * VW).rearrange("p (g n) -> p g n", n=VW) for _ in range(2)] for _ in range(2)]
        probs = [room(HEADS_R * SP).rearrange("p (h s) -> p h s", s=SP) for _ in range(4)]
        row_max = [room(HEADS_R) for _ in range(2)]
        probs_T = [room(4 * P).rearrange("p (j n) -> p j n", j=4) for _ in range(2)]
        rden = [room(HEADS_R) for _ in range(2)]
        o_tok = [room(2 * 2 * 2 * C).rearrange("p (e u b c) -> p e u b c", b=2, e=2, u=2) for _ in range(2)]
        res = [room(UT) for _ in range(2)]

        used[1] = 0
        raw = room(CH * RAW)
        smax, lsum = room(PIX), room(PIX)
        lden = [room(PIX)]
        xh, sc = [], []
        for _ in range(2):
            xh.append(room(HD * HALO).rearrange("p (c h w) -> p c h w", c=HD, h=HR))
            sc.append(room(NK * PIX).rearrange("p (k n) -> p k n", k=NK))
            if len(sc) == 1:
                room(-used[1] % HW % 128)
                early_pairs = used[1] // HW
        raw_first = [raw] + [sc[1].rearrange("p k n -> p (k n)")[:, n * CH * RAW:(n + 1) * CH * RAW] for n in range(3)]
        dve_ring = [room(TILE) for _ in range(SLOTS["dve"])]
        dve_extra = [room(CH * PIX) for _ in range(2)]
        pool_ring = [room(TILE) for _ in range(SLOTS["pool"])]
        lden.append(room(PIX))
        o_loc = room(CH * PIX).rearrange("p (c n) -> p c n", c=CH)
        used[1] = 0
        x1_in = [room(HW) for _ in range(BP)]
        at_in = [room(HW) for _ in range(BP)]

        x_loaded = [sem(f"x_loaded{i}") for i in range(BP)]
        par_loaded = sem("par_loaded")
        w_zeroed = sem("w_zeroed")
        masks_ready = sem("masks_ready")
        bufs_zeroed = sem("bufs_zeroed")
        w_transposed = sem("w_transposed")
        wT_ready = sem("wT_ready")
        st = sem("st")
        gn_in = sem("gn_in")
        gn_out = sem("gn_out")
        sq_in = sem("sq_in")
        sq_out = sem("sq_out")
        affine_ready = sem("affine_ready")
        tok_ready = sem("tok_ready")
        proj_done = sem("proj_done")
        proj_copied = sem("proj_copied")
        kbd_ready = sem("kbd_ready")
        vtr_done = sem("vtr_done")
        vbd_ready = sem("vbd_ready")
        s_done = sem("s_done")
        max_done = sem("max_done")
        sub_done = sem("sub_done")
        exp_done = sem("exp_done")
        pt_done = sem("pt_done")
        pt_copied = sem("pt_copied")
        pv_done = sem("pv_done")
        rden_done = sem("rden_done")
        norm_done = sem("norm_done")
        ot_done = sem("ot_done")
        x1_stats = sem("x1_stats")
        res_ready = sem("res_ready")
        added = sem("added")
        pair_ready = sem("pair_ready")
        sel_done = sem("sel_done")
        row_par_ready = sem("row_par_ready")
        no_rows_ready = sem("no_rows_ready")
        edges_stored = sem("edges_stored")
        pads_zeroed = sem("pads_zeroed")
        x1_stored = sem("x1_stored")
        raw_first_loaded = [sem(f"raw_first_loaded{n}") for n in range(4)]
        raw_loaded = [sem("raw_loaded0"), sem("raw_loaded1")]
        scaled = sem("scaled")
        xh_ready = sem("xh_ready")
        dprod = sem("dprod")
        dprod_used = sem("dprod_used")
        pprod = sem("pprod")
        pprod_used = sem("pprod_used")
        dlink = sem("dlink")
        sc_copied = sem("sc_copied")
        lmax_done = sem("lmax_done")
        lsub_done = sem("lsub_done")
        lexp_done = sem("lexp_done")
        lden_done = sem("lden_done")
        lsum_done = sem("lsum_done")
        out_norm = sem("out_norm")
        o_stored = sem("o_stored")
        x1_reloaded = [sem(f"x1_reloaded{i}") for i in range(BP)]
        attn_loaded = [sem(f"attn_loaded{i}") for i in range(BP)]
        fproj = sem("fproj")
        fin_ready = sem("fin_ready")
        out_stored = sem("out_stored")

        block = ctx.enter_context(nc.Block())

        def unit_pixels(u):
            off = (u // NI) * HW + (u % NI) * W
            first = arena[:, off:off + 1] if isinstance(u, int) else arena[:, bass.ds(off, 1)]
            return bass.AP(first.tensor, first.offset, [list(first.ap[0]), [1, NI], [NI * W, WS], [NI, WS]])

        def of_pair(t, u):
            return t[:, u // NI:u // NI + 1] if isinstance(u, int) else t[:, bass.ds(u // NI, 1)]

        def residue(buf, e, r):
            return buf[:, e * ELT + r:e * ELT + r + 4 * (SP - 1) + 1:4]

        def units(eng, unit, peel=1):
            for u in range(peel):
                unit(u, u % 2, u == 0, False)
            with eng.Fori(0, (UNITS - 1 - peel) // 2) as i:
                unit(peel + 2 * i, peel % 2, False, False)
                unit(peel + 1 + 2 * i, 1 - peel % 2, False, False)
            for u in range(peel + (UNITS - 1 - peel) // 2 * 2, UNITS):
                unit(u, u % 2, False, u == UNITS - 1)

        def heads(eng, iteration, looped=LH - 4):
            iteration(0, 0, True, False, PLANS[0])
            iteration(1, 1, True, True, PLANS[1])
            with eng.Fori(0, looped // 2) as i:
                iteration(2 + 2 * i, 0, True, True, FULL)
                iteration(3 + 2 * i, 1, True, True, FULL)
            for j in range(2 + looped, LH):
                iteration(j, j % 2, True, True, PLANS[j])
            iteration(LH, 0, False, True, PLANS[LH])

        def multiply(eng, task, jp, buf):
            if task[0] == "s":
                _, t, a, _ = task
                dy, dx = HALF_PLANE[t]
                r0, rows, c0, cols = region(dy, dx)
                X = xh[jp][:, a * CH:(a + 1) * CH]
                tile = buf[:, 0:CH * rows * cols].rearrange("p (c h w) -> p c h w", c=CH, h=rows)
                return [(tile, X[:, :, r0:r0 + rows, c0:c0 + cols],
                         X[:, :, r0 + dy:r0 + dy + rows, c0 + dx:c0 + dx + cols])]
            _, half, ks = task
            X = xh[1 - jp][:, half * CH:(half + 1) * CH]
            ops = []
            for m, k in enumerate(ks):
                dst = dve_extra[m % 2] if m else buf[:, 0:CH * PIX]
                dy, dx = ALL_SHIFTS[k]
                weight = sc[1 - jp][:, k, :].rearrange("p (h w) -> p h w", w=W)
                ops.append((dst.rearrange("p (c h w) -> p c h w", c=CH, h=GR),
                            X[:, :, R + dy:R + dy + GR, R + dx:R + dx + W],
                            weight.unsqueeze(1).to_broadcast([P, CH, GR, W])))
            return ops

        def last_tile(steps, match, producers):
            return max(n for n, (who, t) in enumerate(steps) if who in producers and match(t))

        def await_sums(eng, j, steps, match):
            last = last_tile(steps, match, ("dve", "pool"))
            who = steps[last][0]
            eng.wait_ge(dprod_used if who == "dve" else pprod_used,
                        tiles_before(j, who) + count(steps[:last + 1], who))

        def await_products(eng, j, steps, half):
            for who, made in (("dve", dprod), ("pool", pprod)):
                last = last_tile(steps, lambda t: t[:2] == ("v", half), (who,))
                eng.wait_ge(made, tiles_before(j, who) + count(steps[:last + 1], who))

        def await_operands(eng, j, task, seen):
            if task[0] == "s" and task[2] not in seen:
                seen.add(task[2])
                eng.wait_ge(xh_ready, 2 * j + task[2] + 1)
            if task[0] == "v" and "v" not in seen:
                seen.add("v")
                eng.wait_ge(lexp_done, SUB_PARTS * j)

        @block.sync
        def _(sp):
            sp.dma_start(xs[:, 0, :], x_rows[:, 0, :]).then_inc(x_loaded[0], 16)
            sp.wait_ge(w_zeroed, 1)
            for b2 in range(2):
                rows = slice(b2 * C, (b2 + 1) * C)
                sp.dma_start(w_nat[b2][:, rows], qk_w).then_inc(par_loaded, 16)
                sp.dma_start(w_nat[2][rows, rows], v_w).then_inc(par_loaded, 16)
                sp.dma_start(w_nat[3][rows, rows], w_out).then_inc(par_loaded, 16)
                for n, v in enumerate((bn_gamma, bn_beta, bn_mean, bn_var, b_out)):
                    sp.dma_start(par[rows, n:n + 1], v.rearrange("(c o) -> c o", o=1)).then_inc(par_loaded, 16)
            for bp in range(1, BP):
                sp.dma_start(xs[:, bp, :], x_rows[:, bp, :]).then_inc(x_loaded[bp], 16)
            sp.wait_ge(no_rows_ready, 1)
            sp.dma_start(x1_flat[0:1, 0:R * W], no_rows[0:1, :]).then_inc(edges_stored, 16)
            sp.dma_start(x1_flat[0:1, R * W + 2 * C * BP * HW:], no_rows[0:1, :]).then_inc(edges_stored, 16)
            def store_x1(bp):
                sp.wait_ge(added, NI * (bp + 1))
                sp.dma_start(x1_dram[:, bp, :], xs[:, bp, :]).then_inc(x1_stored, 16)

            def load_half(j, a, g0=0, g1=C):
                early = isinstance(j, int) and j < 2
                buf = (raw_first[2 * j + a] if early else raw).rearrange("p (c n) -> p c n", c=CH)
                loaded = raw_first_loaded[2 * j + a] if early else raw_loaded[a]
                for b2 in range(2):
                    off = (b2 * C + j * HD + a * CH) * BP * HW + g0 * PIX
                    at = x1_flat[0:1, off:off + 1] if isinstance(j, int) else x1_flat[0:1, bass.ds(off, 1)]
                    src = bass.AP(at.tensor, at.offset, [[PIX, g1 - g0], [BP * HW, CH], [1, RAW]])
                    sp.dma_start(buf[b2 * C + g0:b2 * C + g1], src).then_inc(loaded, 16)

            def store_half(j, a):
                for b2 in range(2):
                    c0 = j * HD + a * CH
                    dst = attn_dram[b2, c0:c0 + CH] if isinstance(j, int) else attn_dram[b2, bass.ds(c0, CH)]
                    sp.dma_start(dst.rearrange("c bp rg n -> (bp rg) c n"),
                                 o_loc[b2 * C:(b2 + 1) * C]).then_inc(o_stored, 16)

            for bp in range(BP - 1):
                store_x1(bp)
            sp.wait_ge(edges_stored, 32)
            sp.wait_ge(x1_stored, 16 * (BP - 1))
            sp.wait_ge(x1_stats, NI)
            split = (BP - 1) * RG - 1
            load_half(0, 0, 1, split)
            store_x1(BP - 1)
            sp.wait_ge(x1_stored, 16 * BP)
            load_half(0, 0, 0, 1)
            load_half(0, 0, split, C)
            sp.wait_ge(x1_stats, UNITS)
            load_half(0, 1)
            for a in range(2):
                load_half(1, a)

            def reload_x1(bp):
                sp.dma_start(x1_in[bp], x1_dram[:, bp, :]).then_inc(x1_reloaded[bp], 16)

            def iteration(j, jp, do_s, do_v, steps):
                if isinstance(j, int) and j == LH:
                    sp.wait_ge(dprod, tiles_before(LH, "dve"))
                    sp.wait_ge(pprod, tiles_before(LH, "pool"))
                    sp.wait_ge(out_norm, 2 * (LH - 1))
                    sp.wait_ge(lden_done, LH)
                    for bp in range(early_pairs):
                        reload_x1(bp)
                for a in range(2):
                    if do_s and do_v and not (isinstance(j, int) and j + 1 >= LH):
                        sp.wait_ge(xh_ready, 2 * (j + 1) + a)
                        load_half(j + 1, a)
                    if do_v:
                        sp.wait_ge(out_norm, 2 * (j - 1) + a + 1)
                        store_half(j - 1, a)
            heads(sp, iteration)
            sp.wait_ge(o_stored, 16 * 4 * LH)

            for bp in range(BP):
                if bp >= early_pairs:
                    reload_x1(bp)
                sp.dma_start(at_in[bp], attn_rows[:, bp, :]).then_inc(attn_loaded[bp], 16)
            for bp in range(BP):
                sp.wait_ge(fin_ready, 2 * bp + 2)
                sp.dma_start(out_rows[:, bp, :], x1_in[bp]).then_inc(out_stored, 16)
            sp.wait_ge(out_stored, 16 * BP)

        @block.gpsimd
        def _(pool):
            for w in w_nat:
                i = nc.gpsimd.memset(w, 0.0)
            i.then_inc(w_zeroed, 1)
            nc.gpsimd.memset(ident, 0.0)
            nc.gpsimd.memset(pair_mean, 0.5)
            nc.gpsimd.memset(row_sel, 1.0)
            nc.gpsimd.memset(edge_ones, 1.0)
            nc.gpsimd.memset(no_rows, 0.0).then_inc(no_rows_ready, 1)
            nc.gpsimd.memset(head_mask, 1.0).then_inc(masks_ready, 1)
            pool.wait_ge(masks_ready, 1)
            nc.gpsimd.affine_select(out=ident, in_=ident, compare_op=ALU.not_equal, fill=1.0, base=0,
                                    pattern=[[-1, P]], channel_multiplier=1)
            groups = pair_mean.rearrange("p (j k) -> p j k", k=2)
            nc.gpsimd.affine_select(out=groups, in_=groups, compare_op=ALU.is_ge, fill=0.0, base=0,
                                    pattern=[[-2, C], [0, 2]], channel_multiplier=1)
            for n in range(2):
                nc.gpsimd.affine_select(out=row_sel[:, n * C:(n + 1) * C], in_=row_sel[:, n * C:(n + 1) * C],
                                        compare_op=ALU.is_ge, fill=0.0, base=RG * BP * n, pattern=[[1, C]],
                                        channel_multiplier=-RG)
                nc.gpsimd.affine_select(out=edge_ones[:, n * 16:(n + 1) * 16], in_=edge_ones[:, n * 16:(n + 1) * 16],
                                        compare_op=ALU.not_equal, fill=0.0, base=-(RG - 1) * n,
                                        pattern=[[-RG, 16]], channel_multiplier=1)
            slots = head_mask.rearrange("p (j h) -> p j h", h=2)
            nc.gpsimd.affine_select(out=slots, in_=slots, compare_op=ALU.is_ge, fill=0.0, base=0,
                                    pattern=[[-16, 4], [-64, 2]], channel_multiplier=1).then_inc(masks_ready, 1)
            pool.wait_ge(masks_ready, 2)
            for n in range(2):
                nc.gpsimd.affine_select(out=row_sel[:, n * C:(n + 1) * C], in_=row_sel[:, n * C:(n + 1) * C],
                                        compare_op=ALU.is_ge, fill=0.0, base=RG - 1 - RG * BP * n, pattern=[[-1, C]],
                                        channel_multiplier=RG)
            nc.gpsimd.affine_select(out=groups, in_=groups, compare_op=ALU.is_ge, fill=0.0, base=1,
                                    pattern=[[2, C], [0, 2]], channel_multiplier=-1)
            nc.gpsimd.affine_select(out=slots, in_=slots, compare_op=ALU.is_ge, fill=0.0, base=15,
                                    pattern=[[16, 4], [64, 2]], channel_multiplier=-1).then_inc(masks_ready, 1)
            pool.wait_ge(masks_ready, 3)
            for u in range(2):
                for b2 in range(2):
                    nc.gpsimd.memset(qk_sb[u][b2][:, UT:UT + SP], 0.0)
                    nc.gpsimd.memset(v_bd[u][b2], 0.0)
                nc.gpsimd.memset(v_ch[u], 0.0)
            for q in probs:
                i = nc.gpsimd.memset(q, 0.0)
            i.then_inc(bufs_zeroed, 1)
            pool.wait_ge(bufs_zeroed, 1)
            for u in range(2):
                for e in range(2):
                    nc.gpsimd.memset(v_bd[u][e][0:SP, :, 32:33], 1.0)
                    i = nc.gpsimd.memset(v_bd[u][e][SP:P, :, 33:34], 1.0)
            i.then_inc(bufs_zeroed, 1)

            def expand_keys(k, up):
                b2, e = k // 2, k % 2
                for r in range(2):
                    keys = residue(qk_sb[up][b2], e, 2 + r)[:, 0:S]
                    i = nc.gpsimd.tensor_tensor(k_bd[k][:, r], keys.unsqueeze(1).to_broadcast([P, HEADS_R, S]),
                                                head_mask.unsqueeze(2).to_broadcast([P, HEADS_R, S]), ALU.mult)
                i.then_inc(kbd_ready, 1)

            def add_residual(u, up):
                pool.wait_ge(res_ready, 2 * u + 2)
                v = unit_pixels(u)
                nc.gpsimd.tensor_tensor(v, v, res[up].rearrange("p (i a c) -> p i a c", i=NI, a=WS),
                                        ALU.add).then_inc(added, 1)

            def unit(u, up, first, last):
                for k in range(4):
                    if k % 2 == 0:
                        pool.wait_ge(proj_copied, 3 * u + k // 2 + 1)
                    if not first:
                        pool.wait_ge(s_done, 4 * u + k - 3)
                    expand_keys(k, up)
                    if k == 1 and not (isinstance(u, int) and u < 2):
                        add_residual(u - 2, up)
            units(pool, unit, peel=2)
            add_residual(UNITS - 2, 0)
            add_residual(UNITS - 1, 1)

            pool.wait_ge(x1_stored, 16 * BP)
            pool.wait_ge(x1_stats, UNITS)
            for q in xh:
                nc.gpsimd.memset(q[:, :, :, 0:R], 0.0)
                i = nc.gpsimd.memset(q[:, :, :, R + W:WP], 0.0)
            i.then_inc(pads_zeroed, 1)
            pool.wait_ge(pads_zeroed, 1)

            def iteration(j, jp, do_s, do_v, steps):
                n = 0
                seen = set()
                for who, task in steps:
                    if who != "pool":
                        continue
                    await_operands(pool, j, task, seen)
                    if not (isinstance(j, int) and j == 0 and n < SLOTS["pool"]):
                        pool.wait_ge(pprod_used, slot_free(j, n, "pool"))
                    (o, a, b), = multiply(pool, task, jp, pool_ring[n % SLOTS["pool"]])
                    nc.gpsimd.tensor_tensor(o, a, b, ALU.mult).then_inc(pprod, 1)
                    n += 1
            heads(pool, iteration)

        @block.scalar
        def _(act):
            act.wait_ge(wT_ready, 1)
            nc.scalar.activation(bn_inv, bn_off, ACT.Sqrt).then_inc(sq_out, 1)

            def group_roots(turn):
                pairs = PAIRS_OF_TURN[turn]
                act.wait_ge(sq_in, turn + 1)
                nc.scalar.activation(g_dev[:, pairs], g_std[:, pairs], ACT.Sqrt).then_inc(sq_out, 1)

            group_roots(0)
            nc.scalar.preload_act_table(ACT.Exp)
            act.wait_ge(affine_ready, 1)
            act.wait_ge(bufs_zeroed, 2)

            def gather(u, up):
                nc.scalar.activation(tok[up].rearrange("p (i a c) -> p i a c", i=NI, a=WS), unit_pixels(u),
                                     ACT.Identity, bias=of_pair(t_bias, u), scale=of_pair(t_scale, u)
                                     ).then_inc(tok_ready, 1)

            def copy_qk(u, up, b2):
                act.wait_ge(proj_done, 3 * u + b2 + 1)
                nc.scalar.activation(qk_sb[up][b2][:, 0:UT], PS[:, 0, 0:UT], ACT.Copy).then_inc(proj_copied, 1)

            def copy_v(u, up):
                act.wait_ge(proj_done, 3 * u + 3)
                nc.scalar.activation(v_ch[up][:, :, :, 0:S], PS[:, 0, 0:UT].rearrange("p (e s r) -> p e r s", e=2, r=4),
                                     ACT.Relu).then_inc(proj_copied, 1)

            def place_values(u, up, e):
                act.wait_ge(vtr_done, u + 1)
                groups = PS[:, 1, e * 2 * P:(e + 1) * 2 * P].rearrange("p (g n) -> p g n", n=16)
                for h in range(2):
                    rows = slice(h * SP, h * SP + S)
                    i = nc.scalar.activation(v_bd[up][e][rows, :, h * 16:h * 16 + 16], groups[rows], ACT.Copy)
                i.then_inc(vbd_ready, 1)

            def exponentials(n, k):
                act.wait_ge(sub_done, n + 1)
                nc.scalar.activation(probs[k][:, :, 0:S], probs[k][:, :, 0:S], ACT.Exp,
                                     scale=ATT_SCALE).then_inc(exp_done, 1)

            def copy_transposed(n, k, ready=True):
                act.wait_ge(pt_done, n + 1)
                if not (isinstance(n, int) and n < 2):
                    act.wait_ge(pv_done, n - 1)
                nc.scalar.activation(probs_T[k % 2].rearrange("p j n -> p (j n)"), PS[:, 4 + k % 2, :],
                                     ACT.Copy).then_inc(pt_copied, 1)

            gather(0, 0)
            for b2 in range(2):
                copy_qk(0, 0, b2)
            copy_v(0, 0)

            def unit(u, up, first, last):
                for k in range(4):
                    n = 4 * u + k
                    if not (first and k == 0):
                        copy_transposed(n - 1, (k - 1) % 4)
                    exponentials(n, k)
                    if k < 2:
                        place_values(u, up, k)
                    if not last:
                        if k == 0:
                            gather(u + 1, 1 - up)
                        elif k < 3:
                            copy_qk(u + 1, 1 - up, k - 1)
                        else:
                            copy_v(u + 1, 1 - up)
                if isinstance(u, int) and u == STATS_UNIT:
                    group_roots(1)
                    nc.scalar.preload_act_table(ACT.Exp)
                    act.wait_ge(affine_ready, 2)
            units(act, unit, peel=PEEL)
            copy_transposed(4 * UNITS - 1, 3)

            group_roots(2)
            nc.scalar.preload_act_table(ACT.Exp)
            act.wait_ge(row_par_ready, 1)

            def param(n, c):
                return row_par[:, n * C + c:n * C + c + 1] if isinstance(c, int) else \
                    row_par[:, bass.ds(n * C + c, 1)]

            def normalise_half(j, jp, a):
                if isinstance(j, int) and j < 2:
                    act.wait_ge(raw_first_loaded[2 * j + a], 96 if (j, a) == (0, 0) else 32)
                else:
                    act.wait_ge(raw_loaded[a], 32 * (j - 1))
                buf = (raw_first[2 * j + a] if isinstance(j, int) and j < 2 else raw).rearrange("p (c n) -> p c n", c=CH)
                for c in range(CH):
                    chan = j * HD + a * CH + c
                    i = nc.scalar.activation(xh[jp][:, a * CH + c, :, R:R + W],
                                             buf[:, c, :].rearrange("p (h w) -> p h w", w=W),
                                             ACT.Identity, bias=param(1, chan), scale=param(0, chan))
                i.then_inc(scaled, 1)
                act.wait_ge(scaled, 2 * j + a + 1)
                for n, h in enumerate((0, R + GR)):
                    rows = xh[jp][:, a * CH:(a + 1) * CH, h:h + R, R:R + W]
                    i = nc.scalar.activation(rows, rows, ACT.Copy, scale=edge[:, n:n + 1])
                i.then_inc(xh_ready, 1)

            def copy_scores(j, jp, t, steps):
                await_sums(act, j, steps, lambda task: task[:2] == ("s", t))
                dy, dx = HALF_PLANE[t]
                r0, rows, c0, cols = region(dy, dx)
                segs = segments(rows, cols)
                for sy, sx, py, px in {(dy, dx, 0, 0), (-dy, -dx, -dy, -dx)}:
                    top, left = R + py - r0, R + px - c0
                    dst = sc[jp][:, slot_of(sy, sx), :].rearrange("p (h w) -> p h w", w=W)
                    for s, (a, b) in enumerate(segs):
                        lo, hi = max(a, top), min(b, top + GR)
                        if lo >= hi:
                            continue
                        src = PS[:, 2 * (t % 2) + s, 0:(b - a) * cols].rearrange("p (h w) -> p h w", w=cols)
                        i = nc.scalar.activation(dst[:, lo - top:hi - top], src[:, lo - a:hi - a, left:left + W],
                                                 ACT.Copy)
                i.then_inc(sc_copied, 1)

            def iteration(j, jp, do_s, do_v, steps):
                if not do_s:
                    return
                if isinstance(j, int) and j == 0:
                    for a in range(2):
                        normalise_half(0, 0, a)
                else:
                    act.wait_ge(dprod, tiles_before(j, "dve"))
                    act.wait_ge(pprod, tiles_before(j, "pool"))
                for kind, task in steps:
                    if kind == "copy":
                        copy_scores(j, jp, task, steps)
                        if isinstance(j, int) and j == 0 and task in (4, 8):
                            normalise_half(1, 1, task // 8)
                    elif kind == "exp":
                        offset, m = task
                        act.wait_ge(lsub_done, SUB_PARTS * (j - offset) + m + 1)
                        v = sc[(jp + offset) % 2][:, m * KS:(m + 1) * KS, :].rearrange("p k n -> p (k n)")
                        nc.scalar.activation(v, v, ACT.Exp).then_inc(lexp_done, 1)
                    elif kind == "pixels" and not (isinstance(j, int) and j + 1 >= LH):
                        await_products(act, j, steps, task)
                        normalise_half(j + 1, 1 - jp, task)
            heads(act, iteration)

        @block.vector
        def _(dve):
            steps = [0]

            def step(i):
                steps[0] += 1
                i.then_inc(st, 1)
                dve.wait_ge(st, steps[0])

            def group_stats(stage, turn, chunks):
                b0, b1 = PAIRS_OF_TURN[turn].start, PAIRS_OF_TURN[turn].stop
                mean, var = mean_var[:, b0:b1, 0], mean_var[:, b0:b1, 1]
                g_m, g_d, g_s, tmp = (t[:, b0:b1] for t in (g_mean, g_dev, g_std, t_tmp))
                paired = PS[:, 1, b0:b1]
                if stage == 0:
                    for bp in range(b0, b1):
                        i = nc.vector.bn_aggr(mean_var[:, bp, :], chunk_stats[:, bp * chunks * 6:(bp + 1) * chunks * 6])
                    step(i)
                    nc.vector.tensor_copy(tmp, mean).then_inc(gn_in, 1)
                elif stage == 1:
                    dve.wait_ge(gn_out, 2 * turn + 1)
                    step(nc.vector.tensor_copy(g_m, paired))
                    step(nc.vector.tensor_tensor(g_d, mean, g_m, ALU.subtract))
                    step(nc.vector.tensor_tensor(g_s, g_d, g_d, ALU.mult))
                    nc.vector.tensor_tensor(tmp, g_s, var, ALU.add).then_inc(gn_in, 1)
                elif stage == 2:
                    dve.wait_ge(gn_out, 2 * turn + 2)
                    nc.vector.tensor_scalar(g_s, paired, GN_EPS, None, ALU.add).then_inc(sq_in, 1)
                else:
                    dve.wait_ge(sq_out, turn + 2)
                    step(nc.vector.reciprocal(g_rstd[:, b0:b1], g_d))
                    return nc.vector.scalar_tensor_tensor(out=g_bias[:, b0:b1], in0=g_m, scalar=-1.0,
                                                          in1=g_rstd[:, b0:b1], op0=ALU.mult, op1=ALU.mult)

            def stats(chunks):
                for n in chunks:
                    if n % CHUNKS == 0:
                        dve.wait_ge(x_loaded[n // CHUNKS], 16)
                    w = HW // CHUNKS
                    i = nc.vector.bn_stats(chunk_stats[:, 6 * n:6 * n + 6],
                                           xs[:, n // CHUNKS, n % CHUNKS * w:(n % CHUNKS + 1) * w])
                return i

            def affine(i, pairs):
                step(i)
                nc.vector.tensor_scalar(t_scale[:, pairs], g_rstd[:, pairs], bn_inv, None, ALU.mult)
                nc.vector.tensor_scalar(t_bias[:, pairs], g_bias[:, pairs], bn_inv, bn_off, ALU.mult,
                                        ALU.add).then_inc(affine_ready, 1)

            step(stats(range(CHUNKS)))
            dve.wait_ge(par_loaded, 16 * 16)
            dve.wait_ge(masks_ready, 3)
            nc.vector.tensor_scalar(bn_off, par[:, 3:4], BN_EPS, None, ALU.add).then_inc(wT_ready, 1)
            dve.wait_ge(w_transposed, 1)
            nc.vector.tensor_copy(w_T_all, PS[:, 1, :]).then_inc(wT_ready, 1)
            dve.wait_ge(sq_out, 1)
            step(nc.vector.reciprocal(bn_off, bn_inv))
            step(nc.vector.tensor_tensor(bn_inv, bn_off, par[:, 0:1], ALU.mult))
            step(nc.vector.tensor_tensor(t_tmp[:, 0:1], par[:, 2:3], bn_inv, ALU.mult))
            step(nc.vector.tensor_tensor(bn_off, par[:, 1:2], t_tmp[:, 0:1], ALU.subtract))
            for n in range(2):
                nc.vector.tensor_reduce(edge[:, n:n + 1], edge_ones[:, n * 16:(n + 1) * 16], AX_X, ALU.min)
            step(nc.vector.memset(t_tmp, 0.0))
            for stage in range(4):
                i = group_stats(stage, 0, CHUNKS)
            affine(i, PAIRS_OF_TURN[0])
            dve.wait_ge(bufs_zeroed, 2)

            def subtract_max(n, k):
                bank = PS[:, 2 + k % 2, :].rearrange("p (h s) -> p h s", s=SP)[:, :, 0:S]
                dve.wait_ge(s_done, n + 1)
                nc.vector.tensor_reduce(row_max[k % 2], bank, AX_X, ALU.max).then_inc(max_done, 1)
                dve.wait_ge(max_done, n + 1)
                if not (isinstance(n, int) and n < 4):
                    dve.wait_ge(pt_done, n - 3)
                nc.vector.tensor_tensor(probs[k][:, :, 0:S], bank,
                                        row_max[k % 2].unsqueeze(2).to_broadcast([P, HEADS_R, S]),
                                        ALU.subtract).then_inc(sub_done, 1)

            def normalise(n, k, up):
                b2, e = k // 2, k % 2
                rd = rden[k % 2].rearrange("p (j q) -> p j q", q=2)
                o = PS[:, 6, 0:8 * VW].rearrange("p (j r n) -> p j r n", j=4, r=2)
                dve.wait_ge(pv_done, n + 1)
                nc.vector.reciprocal(rd, o[:, :, 0, 32:34]).then_inc(rden_done, 1)
                dve.wait_ge(rden_done, n + 1)
                for r in range(2):
                    rows = slice(r * SP, (r + 1) * SP)
                    dst = o_tok[up][rows, e, :, b2, :].rearrange("p q (j d) -> p j q d", j=4)
                    i = nc.vector.tensor_tensor(dst, o[rows, :, r, 0:32].rearrange("p j (q d) -> p j q d", q=2),
                                                rd[rows].unsqueeze(3).to_broadcast([SP, 4, 2, 16]), ALU.mult)
                i.then_inc(norm_done, 1)

            def order_tokens(u, up):
                dve.wait_ge(ot_done, u + 1)
                if not (isinstance(u, int) and u < 2):
                    dve.wait_ge(added, u - 1)
                for e in range(2):
                    src = PS[:, 7, e * 2 * P:(e + 1) * 2 * P].rearrange("p (h r s) -> p h r s", h=2, r=2)[:, :, :, 0:S]
                    dst = res[up][:, e * ELT:(e + 1) * ELT].rearrange("p (s r h) -> p h r s", r=2, h=2)
                    nc.vector.tensor_copy(dst, src).then_inc(res_ready, 1)

            def unit(u, up, first, last):
                for k in range(4):
                    n = 4 * u + k
                    subtract_max(n, k)
                    if not (first and k < 2):
                        normalise(n - 2, (k - 2) % 4, up if k >= 2 else 1 - up)
                    if k == 3 and not first:
                        order_tokens(u - 1, 1 - up)
                    if k == 3 and not (isinstance(u, int) and u < 3):
                        unit_stats(u - 3)
                    if isinstance(u, int) and u < STATS_UNIT:
                        step(stats(STATS_OF[n]))
                    if isinstance(u, int) and u == STATS_UNIT and k >= 1:
                        i = group_stats(k - 1, 1, CHUNKS)
                        if k == 3:
                            affine(group_stats(3, 1, CHUNKS), PAIRS_OF_TURN[1])

            def unit_stats(u):
                s = chunk_stats[:, 6 * u:6 * u + 6] if isinstance(u, int) else chunk_stats[:, bass.ds(6 * u, 6)]
                nc.vector.bn_stats(s, unit_pixels(u)).then_inc(x1_stats, 1)
            units(dve, unit, peel=PEEL)
            normalise(4 * UNITS - 2, 2, 1)
            normalise(4 * UNITS - 1, 3, 1)
            order_tokens(UNITS - 1, 1)

            for u in range(UNITS - 3, UNITS):
                dve.wait_ge(added, u + 1)
                unit_stats(u)
            dve.wait_ge(x1_stats, UNITS)
            for stage in range(4):
                i = group_stats(stage, 2, NI)
            i.then_inc(pair_ready, 1)
            dve.wait_ge(sel_done, 1)
            nc.vector.tensor_copy(pair_T[0:2 * BP], PS[0:2 * BP, 1, 0:P]).then_inc(pair_ready, 1)
            dve.wait_ge(sel_done, 2)
            nc.vector.tensor_copy(row_par, PS[:, 2, 0:2 * C]).then_inc(row_par_ready, 1)
            dve.wait_ge(pads_zeroed, 1)

            def norm_half(j, jp, a):
                if not (isinstance(j, int) and j == 0 and a == 0):
                    dve.wait_ge(o_stored, 64 * j + 32 * a)
                nc.vector.tensor_tensor(o_loc, PS[:, 4:8, 0:PIX],
                                        lden[jp].unsqueeze(1).to_broadcast([P, CH, PIX]),
                                        ALU.mult).then_inc(out_norm, 1)

            def softmax_step(j, jp, m):
                w = PIX // MAX_PARTS
                if m < MAX_PARTS:
                    if m == 0:
                        dve.wait_ge(sc_copied, S_TILES * (j + 1))
                    nc.vector.tensor_reduce(smax[:, m * w:(m + 1) * w],
                                            sc[jp][:, :, m * w:(m + 1) * w].rearrange("p k n -> p n k"),
                                            AX_X, ALU.max).then_inc(lmax_done, 1)
                    return
                m -= MAX_PARTS
                if m < SUB_PARTS:
                    if m == 0:
                        dve.wait_ge(lmax_done, MAX_PARTS * (j + 1))
                    v = sc[jp][:, m * KS:(m + 1) * KS, :]
                    nc.vector.tensor_tensor(v, v, smax.unsqueeze(1).to_broadcast([P, KS, PIX]),
                                            ALU.subtract).then_inc(lsub_done, 1)
                    return
                m -= SUB_PARTS
                if m < MAX_PARTS:
                    if m == 0:
                        dve.wait_ge(lexp_done, SUB_PARTS * (j + 1))
                    nc.vector.tensor_reduce(lsum[:, m * w:(m + 1) * w],
                                            sc[jp][:, :, m * w:(m + 1) * w].rearrange("p k n -> p n k"),
                                            AX_X, ALU.add).then_inc(lsum_done, 1)
                    return
                dve.wait_ge(lsum_done, MAX_PARTS * (j + 1))
                nc.vector.reciprocal(lden[jp], lsum).then_inc(lden_done, 1)

            def iteration(j, jp, do_s, do_v, steps):
                n, done = 0, tiles_before(j, "dve")
                linked = before(j, links)
                seen = set()
                for who, task in steps:
                    if who == "norm":
                        offset, half = task
                        dve.wait_ge(lden_done, j - offset + 1)
                        if offset == 1:
                            await_sums(dve, j, steps, lambda t: t[:2] == ("v", half))
                        else:
                            dve.wait_ge(dprod_used, tiles_before(j, "dve"))
                            dve.wait_ge(pprod_used, tiles_before(j, "pool"))
                        norm_half(j - offset, (jp + offset) % 2, half)
                    if who == "soft":
                        offset, m = task
                        softmax_step(j - offset, (jp + offset) % 2, m)
                    if who != "dve":
                        continue
                    await_operands(dve, j, task, seen)
                    if not (isinstance(j, int) and j == 0 and n < SLOTS["dve"]):
                        dve.wait_ge(dprod_used, slot_free(j, n, "dve"))
                    buf = dve_ring[n % SLOTS["dve"]]
                    ops = multiply(dve, task, jp, buf)
                    if task[0] == "s":
                        _, rows, _, cols = region(*HALF_PLANE[task[1]])
                        w = CH // 2 * rows * cols
                        nc.vector.tensor_tensor(*ops[0], ALU.mult).then_inc(dlink, 1)
                        linked += 1
                        dve.wait_ge(dlink, linked)
                        nc.vector.tensor_tensor(buf[:, 0:w], buf[:, 0:w], buf[:, w:2 * w], ALU.add).then_inc(dprod, 1)
                    elif len(ops) == 1:
                        nc.vector.tensor_tensor(*ops[0], ALU.mult).then_inc(dprod, 1)
                    else:
                        total = buf[:, 0:CH * PIX]
                        nc.vector.tensor_tensor(*ops[0], ALU.mult).then_inc(dlink, 1)
                        dve.wait_ge(dprod, done + n)
                        nc.vector.tensor_tensor(*ops[1], ALU.mult).then_inc(dlink, 1)
                        linked += 2
                        summed = linked
                        for m in range(1, len(ops)):
                            if m + 1 < len(ops):
                                if m > 1:
                                    dve.wait_ge(dlink, summed)
                                nc.vector.tensor_tensor(*ops[m + 1], ALU.mult).then_inc(dlink, 1)
                                linked += 1
                            dve.wait_ge(dlink, summed)
                            i = nc.vector.tensor_tensor(total, total, dve_extra[m % 2], ALU.add)
                            if m + 1 < len(ops):
                                i.then_inc(dlink, 1)
                                linked += 1
                                summed = linked
                            else:
                                i.then_inc(dprod, 1)
                    n += 1
            heads(dve, iteration)

            for bp in range(BP):
                dve.wait_ge(x1_reloaded[bp], 16)
                for g in range(2):
                    dve.wait_ge(fproj, 2 * bp + g + 1)
                    x1_part = x1_in[bp][:, g * 4 * PIX:(g + 1) * 4 * PIX].rearrange("p (k n) -> p k n", k=4)
                    nc.vector.scalar_tensor_tensor(out=x1_part, in0=PS[:, 4 * g:4 * g + 4, 0:PIX],
                                                   scalar=par[:, 4:5], in1=x1_part,
                                                   op0=ALU.add, op1=ALU.add).then_inc(fin_ready, 1)

        @block.tensor
        def _(pe):
            pe.wait_ge(masks_ready, 3)
            pe.wait_ge(par_loaded, 16 * 16)
            for n, w in enumerate(w_nat):
                i = nc.tensor.transpose(PS[:, 1, n * P:(n + 1) * P], w, ident)
            i.then_inc(w_transposed, 1)

            def pair_means(turn, k):
                pe.wait_ge(gn_in, 2 * turn + k + 1)
                nc.tensor.matmul(PS[:, 1, 0:BP], pair_mean, t_tmp, start=True, stop=True).then_inc(gn_out, 1)

            pe.wait_ge(wT_ready, 2)
            for k in range(2):
                pair_means(0, k)

            def project_qk(u, up, b2):
                if b2 == 0:
                    pe.wait_ge(tok_ready, u + 1)
                if not (isinstance(u, int) and u == 0 and b2 == 0):
                    pe.wait_ge(proj_copied, 3 * u + b2)
                nc.tensor.matmul(PS[:, 0, 0:UT], wqk_T[b2], tok[up], start=True, stop=True).then_inc(proj_done, 1)

            def project_v(u, up):
                pe.wait_ge(proj_copied, 3 * u + 2)
                nc.tensor.matmul(PS[:, 0, 0:UT], wv_T, tok[up], start=True, stop=True).then_inc(proj_done, 1)

            def transpose_v(u, up):
                pe.wait_ge(proj_copied, 3 * u + 3)
                if not (isinstance(u, int) and u == 0):
                    pe.wait_ge(vbd_ready, 2 * u)
                for e in range(2):
                    for r in range(2):
                        i = nc.tensor.transpose(PS[:, 1, (2 * e + r) * P:(2 * e + r + 1) * P],
                                                v_ch[up][:, e, 2 * r:2 * r + 2, :].rearrange("p r s -> p (r s)"), ident)
                i.then_inc(vtr_done, 1)

            def scores(n, k, up):
                b2, e = k // 2, k % 2
                pe.wait_ge(kbd_ready, n + 1)
                if not (isinstance(n, int) and n < 2):
                    pe.wait_ge(sub_done, n - 1)
                for r in range(2):
                    dst = PS[r * SP:(r + 1) * SP, 2 + k % 2, :].rearrange("p (h s) -> p h s", s=SP)[:, :, 0:S]
                    i = nc.tensor.matmul(dst, residue(qk_sb[up][b2], e, r), k_bd[k][:, r], start=True, stop=True)
                i.then_inc(s_done, 1)

            def transpose_probs(n, k):
                pe.wait_ge(exp_done, n + 1)
                if not (isinstance(n, int) and n < 2):
                    pe.wait_ge(pt_copied, n - 1)
                for j in range(4):
                    i = nc.tensor.transpose(PS[:, 4 + k % 2, j * P:(j + 1) * P],
                                            probs[k][:, 2 * j:2 * j + 2, :].rearrange("p h s -> p (h s)"), ident)
                i.then_inc(pt_done, 1)

            def weigh_values(n, k, up, vbd):
                b2, e = k // 2, k % 2
                pe.wait_ge(pt_copied, n + 1)
                pe.wait_ge(vbd_ready, vbd)
                if not (isinstance(n, int) and n == 0):
                    pe.wait_ge(norm_done, n)
                for j in range(4):
                    g = b2 * 4 + j
                    i = nc.tensor.matmul(PS[:, 6, 2 * VW * j:2 * VW * (j + 1)], probs_T[k % 2][:, j, :],
                                         v_bd[up][e][:, g:g + 9:8, :], start=True, stop=True)
                i.then_inc(pv_done, 1)

            def transpose_output(u, up):
                pe.wait_ge(norm_done, 4 * u + 4)
                if not (isinstance(u, int) and u == 0):
                    pe.wait_ge(res_ready, 2 * u)
                for e in range(2):
                    for h in range(2):
                        q = 2 * e + h
                        i = nc.tensor.transpose(PS[:, 7, q * P:(q + 1) * P], o_tok[up][:, e, h].rearrange("p b c -> p (b c)"), ident)
                i.then_inc(ot_done, 1)

            for b2 in range(2):
                project_qk(0, 0, b2)
            project_v(0, 0)

            def unit(u, up, first, last):
                for k in range(4):
                    n = 4 * u + k
                    scores(n, k, up)
                    if k == 0:
                        transpose_v(u, up)
                    if not (first and k == 0):
                        transpose_probs(n - 1, (k - 1) % 4)
                    if not (first and k < 2):
                        m = (k - 2) % 4
                        weigh_values(n - 2, m, up if k >= 2 else 1 - up,
                                     2 * u + m % 2 + 1 - (0 if k >= 2 else 2))
                    if not last:
                        if k in (1, 2):
                            project_qk(u + 1, 1 - up, k - 1)
                        elif k == 3:
                            project_v(u + 1, 1 - up)
                    if k == 3 and not first:
                        transpose_output(u - 1, 1 - up)
                    if isinstance(u, int) and u == STATS_UNIT and k >= 2:
                        pe.wait_ge(vbd_ready, 2 * u + 2)
                        pair_means(1, k - 2)
                if isinstance(u, int) and u == STATS_UNIT:
                    pe.wait_ge(sq_in, 2)
            units(pe, unit, peel=PEEL)
            transpose_probs(4 * UNITS - 1, 3)
            for k in (2, 3):
                weigh_values(4 * UNITS - 4 + k, k, 1, 2 * UNITS)
            transpose_output(UNITS - 1, 1)
            for k in range(2):
                pair_means(2, k)
            pe.wait_ge(pair_ready, 1)
            nc.tensor.transpose(PS[0:2 * BP, 1, 0:P], g_pair, ident).then_inc(sel_done, 1)
            pe.wait_ge(pair_ready, 2)
            for n in range(2):
                for b2 in range(2):
                    i = nc.tensor.matmul(PS[b2 * C:(b2 + 1) * C, 2, n * C:(n + 1) * C], row_sel[0:2 * BP, n * C:(n + 1) * C],
                                         pair_T[0:2 * BP, b2 * C:(b2 + 1) * C], start=True, stop=True)
            i.then_inc(sel_done, 1)

            def iteration(j, jp, do_s, do_v, steps):
                made = {"dve": tiles_before(j, "dve"), "pool": tiles_before(j, "pool")}
                n = {"dve": 0, "pool": 0}
                tiles = [step for step in steps if step[0] in ("dve", "pool")]
                sums = {}
                for _, task in tiles:
                    sums.setdefault(task[:2], []).append(task)
                for who, task in tiles:
                    first, last = task == sums[task[:2]][0], task == sums[task[:2]][-1]
                    ring, ready, used_up = (dve_ring, dprod, dprod_used) if who == "dve" else \
                        (pool_ring, pprod, pprod_used)
                    buf = ring[n[who] % SLOTS[who]]
                    n[who] += 1
                    pe.wait_ge(ready, made[who] + n[who])
                    if task[0] == "s":
                        _, t, a, folded = task
                        chans = CH // 2 if folded else CH
                        _, rows, _, cols = region(*HALF_PLANE[t])
                        if first and not (isinstance(j, int) and j == 0 and t < 2):
                            pe.wait_ge(sc_copied, S_TILES * j + copies_until(steps, t - 2))
                        for c in range(chans):
                            for s, (lo, hi) in enumerate(segments(rows, cols)):
                                i = nc.tensor.matmul(
                                    PS[:, 2 * (t % 2) + s, 0:(hi - lo) * cols], ident,
                                    buf[:, (c * rows + lo) * cols:(c * rows + hi) * cols],
                                    start=(first and c == 0), stop=(last and c == chans - 1))
                        i.then_inc(used_up, 1)
                    else:
                        _, half, ks = task
                        if first and not (isinstance(j, int) and j == 1 and half == 0):
                            pe.wait_ge(out_norm, 2 * (j - 1) + half)
                        for c in range(CH):
                            i = nc.tensor.matmul(PS[:, 4 + c, 0:PIX], ident, buf[:, c * PIX:(c + 1) * PIX],
                                                 start=first, stop=last)
                        i.then_inc(used_up, 1)
            heads(pe, iteration)

            for bp in range(BP):
                pe.wait_ge(attn_loaded[bp], 16)
                for g in range(2):
                    if bp:
                        pe.wait_ge(fin_ready, 2 * bp + g - 1)
                    for k in range(4 * g, 4 * g + 4):
                        i = nc.tensor.matmul(PS[:, k, 0:PIX], wout_T, at_in[bp][:, k * PIX:(k + 1) * PIX],
                                             start=True, stop=True)
                    i.then_inc(fproj, 1)


_INS = ["x", "L0_conv_bn_gamma", "L0_conv_bn_beta", "L0_conv_bn_mean", "L0_conv_bn_var", "L0_conv_qk_w",
        "L0_conv_v_w", "L1_conv_w_out", "L1_conv_b_out"]


def kernel(**inputs):
    import numpy as _np
    import concourse.bacc as _bacc
    from concourse import mybir as _mybir
    from concourse.bass_utils import run_bass_kernel_spmd as _run

    nc = _bacc.Bacc("TRN2", target_bir_lowering=False, num_devices=1)
    arrays, args = {}, []
    for name in _INS:
        a = _np.ascontiguousarray(inputs[name])
        arrays[f"in_{name}_dram"] = a
        args.append(nc.dram_tensor(f"in_{name}_dram", a.shape, _mybir.dt.from_np(a.dtype), kind="ExternalInput").ap())
    args.append(nc.dram_tensor("out_dram", (B, C, H, W), _mybir.dt.float32, kind="ExternalOutput").ap())
    build(nc, *args)
    r = _run(nc, [arrays], core_ids=[0])
    return r.results[0]["out_dram"]
```
